# Optimizing a Trainium2 kernel written in Bass

```python
import numpy as np
import jax
import jax.numpy as jnp

def _softmax(x, axis=-1):
    return jax.nn.softmax(x, axis=axis)

def _gelu(x):
    return jax.nn.gelu(x, approximate=True)

def _silu(x):
    return jax.nn.silu(x)

def _sigmoid(x):
    return jax.nn.sigmoid(x)

def _layernorm(x, axis=-1, eps=1e-05):
    m = jnp.mean(x, axis=axis, keepdims=True)
    v = jnp.var(x, axis=axis, keepdims=True)
    return (x - m) / jnp.sqrt(v + eps)

def _scatter_add(tgt, idx, src, axis=0):
    return tgt.at[idx].add(src)

def _segment_sum(src, seg, n):
    return jax.ops.segment_sum(src, seg, n)
kernel_name = 'mk_hybrid_d1_jaxref_r8_bcc887'

def setup_inputs(seed: int=0):
    np.random.seed(seed)
    _w = jnp.asarray

    def _L0_attn_a_setup():
        import jax, jax.numpy as jnp
        import numpy as np
        B, S, D = (2, 256, 128)
        H, DQ, DV = (16, 64, 64)
        key = jax.random.key(seed)
        k1, k2, k3, k4, k5 = jax.random.split(key, 5)
        scale = 0.02
        return {'x': jax.random.normal(k1, (B, S, D), dtype=jnp.float32), 'w_q': jax.random.normal(k2, (H, DQ, D), dtype=jnp.float32) * scale, 'w_k': jax.random.normal(k3, (H, DQ, D), dtype=jnp.float32) * scale, 'w_v': jax.random.normal(k4, (H, DV, D), dtype=jnp.float32) * scale, 'w_o': jax.random.normal(k5, (D, H * DV), dtype=jnp.float32) * scale}
    _L0_attn_a_in = _L0_attn_a_setup()

    def _L0_attn_b_setup():
        import jax, jax.numpy as jnp
        import numpy as np
        import math
        INPUT_WIDTH = 128
        KEY_WIDTH = 64
        VALUE_WIDTH = 64
        NUM_HEADS = 16
        key = jax.random.key(seed)
        k_x, k_q, k_k, k_v, k_p = jax.random.split(key, 5)
        n, s = (2, 256)
        scale = 1.0 / math.sqrt(INPUT_WIDTH)
        X = jax.random.normal(k_x, (n, s, INPUT_WIDTH), dtype=jnp.float32)
        Wq = jax.random.uniform(k_q, (INPUT_WIDTH, NUM_HEADS * KEY_WIDTH), jnp.float32, -scale, scale)
        Wk = jax.random.uniform(k_k, (INPUT_WIDTH, NUM_HEADS * KEY_WIDTH), jnp.float32, -scale, scale)
        Wv = jax.random.uniform(k_v, (INPUT_WIDTH, NUM_HEADS * VALUE_WIDTH), jnp.float32, -scale, scale)
        p_scale = 1.0 / math.sqrt(NUM_HEADS * VALUE_WIDTH)
        Wpost = jax.random.uniform(k_p, (NUM_HEADS * VALUE_WIDTH, INPUT_WIDTH), jnp.float32, -p_scale, p_scale)
        return {'X': X, 'Wq': Wq, 'Wk': Wk, 'Wv': Wv, 'Wpost': Wpost}
    _L0_attn_b_in = _L0_attn_b_setup()

    def _L0_ffn_setup():
        import jax, jax.numpy as jnp
        import numpy as np
        B, S, D = (2, 256, 128)
        E, K, F = (16, 2, 64)
        FS = 128
        key = jax.random.key(seed)
        ks = jax.random.split(key, 8)

        def w(k, shape, fan_in):
            return jax.random.normal(k, shape, jnp.float32) / np.sqrt(fan_in).astype(np.float32)
        return {'x': jax.random.normal(ks[0], (B, S, D), jnp.float32), 'Wr': w(ks[1], (D, E), D), 'Wg': w(ks[2], (E, D, F), D), 'Wu': w(ks[3], (E, D, F), D), 'Wd': w(ks[4], (E, F, D), F), 'Sg': w(ks[5], (D, FS), D), 'Su': w(ks[6], (D, FS), D), 'Sd': w(ks[7], (FS, D), FS)}
    _L0_ffn_in = _L0_ffn_setup()
    _d = {'L0_attn_a_x': _L0_attn_a_in['x'], 'L0_attn_a_w_q': _L0_attn_a_in['w_q'], 'L0_attn_a_w_k': _L0_attn_a_in['w_k'], 'L0_attn_a_w_v': _L0_attn_a_in['w_v'], 'L0_attn_a_w_o': _L0_attn_a_in['w_o'], 'L0_attn_b_Wq': _L0_attn_b_in['Wq'], 'L0_attn_b_Wk': _L0_attn_b_in['Wk'], 'L0_attn_b_Wv': _L0_attn_b_in['Wv'], 'L0_attn_b_Wpost': _L0_attn_b_in['Wpost'], 'L0_ffn_Wr': _L0_ffn_in['Wr'], 'L0_ffn_Wg': _L0_ffn_in['Wg'], 'L0_ffn_Wu': _L0_ffn_in['Wu'], 'L0_ffn_Wd': _L0_ffn_in['Wd'], 'L0_ffn_Sg': _L0_ffn_in['Sg'], 'L0_ffn_Su': _L0_ffn_in['Su'], 'L0_ffn_Sd': _L0_ffn_in['Sd']}
    _x0 = _d['L0_attn_a_x']
    _d['L0_attn_a_x'] = jax.random.normal(jax.random.fold_in(jax.random.key(seed), 1), (16, 256, 128), dtype=_x0.dtype)
    del _x0
    return _d

def reference(L0_attn_a_x, L0_attn_a_w_q, L0_attn_a_w_k, L0_attn_a_w_v, L0_attn_a_w_o, L0_attn_b_Wq, L0_attn_b_Wk, L0_attn_b_Wv, L0_attn_b_Wpost, L0_ffn_Wr, L0_ffn_Wg, L0_ffn_Wu, L0_ffn_Wd, L0_ffn_Sg, L0_ffn_Su, L0_ffn_Sd):

    def _L0_attn_a_ref(x, w_q, w_k, w_v, w_o):
        import jax, jax.numpy as jnp
        import numpy as np
        B, S, D = (2, 256, 128)
        H, DQ, DV = (16, 64, 64)
        b, s, d = x.shape
        q = jnp.einsum('bsd,hqd->bhsq', x, w_q)
        k = jnp.einsum('bsd,hqd->bhsq', x, w_k)
        v = jnp.einsum('bsd,hvd->bhsv', x, w_v)
        scores = jnp.einsum('bhsq,bhtq->bhst', q, k)
        causal = jnp.triu(jnp.ones((s, s), dtype=bool), k=1)
        masked = jnp.where(causal, -jnp.inf, scores)
        dq = w_q.shape[1]
        weights = jax.nn.softmax(masked / jnp.sqrt(jnp.float32(dq)), axis=-1)
        out = jnp.einsum('bhst,bhtv->bhsv', weights, v)
        cat = out.transpose(0, 2, 1, 3).reshape(b, s, -1)
        return jnp.einsum('bsf,df->bsd', cat, w_o)

    def _L0_attn_b_ref(X, Wq, Wk, Wv, Wpost):
        import jax, jax.numpy as jnp
        import numpy as np
        import math
        INPUT_WIDTH = 128
        KEY_WIDTH = 64
        VALUE_WIDTH = 64
        NUM_HEADS = 16
        n, s, _ = X.shape
        Q = (X @ Wq).reshape(n, s, NUM_HEADS, KEY_WIDTH)
        K = (X @ Wk).reshape(n, s, NUM_HEADS, KEY_WIDTH)
        V = (X @ Wv).reshape(n, s, NUM_HEADS, VALUE_WIDTH)
        inv_sqrt_d = 1.0 / math.sqrt(KEY_WIDTH)
        raw_attn = jnp.einsum('bshe,bthe->bsth', Q, K * inv_sqrt_d)
        attn = jax.nn.softmax(raw_attn, axis=2)
        A = jnp.einsum('bsth,bthe->bshe', attn, V).reshape(n, s, NUM_HEADS * VALUE_WIDTH)
        A = jax.nn.gelu(A, approximate=False)
        P = A @ Wpost
        return X + P

    def _L0_ffn_ref(x, Wr, Wg, Wu, Wd, Sg, Su, Sd):
        import jax, jax.numpy as jnp
        import numpy as np
        B, S, D = (2, 256, 128)
        E, K, F = (16, 2, 64)
        FS = 128
        b, s, d = x.shape
        T = b * s
        xf = x.reshape(T, d)
        shared = jax.nn.silu(xf @ Sg) * (xf @ Su) @ Sd
        probs = jax.nn.softmax(xf @ Wr, axis=-1)
        topk_p, topk_i = jax.lax.top_k(probs, K)
        n_exp = Wr.shape[1]
        cw = jnp.zeros((T, n_exp), x.dtype).at[jnp.arange(T)[:, None], topk_i].add(topk_p)

        def step(acc, ew):
            wg, wu, wd, c = ew
            y = jax.nn.silu(xf @ wg) * (xf @ wu) @ wd
            return (acc + y * c[:, None], None)
        routed, _ = jax.lax.scan(step, jnp.zeros_like(xf), (Wg, Wu, Wd, cw.T))
        return (routed + shared).reshape(b, s, d)
    x = L0_attn_a_x
    x = x + _L0_attn_a_ref(_layernorm(x, axis=-1), L0_attn_a_w_q, L0_attn_a_w_k, L0_attn_a_w_v, L0_attn_a_w_o)
    x = x + _L0_ffn_ref(_layernorm(x, axis=-1), L0_ffn_Wr, L0_ffn_Wg, L0_ffn_Wu, L0_ffn_Wd, L0_ffn_Sg, L0_ffn_Su, L0_ffn_Sd)
    x = x + _L0_attn_b_ref(_layernorm(x, axis=-1), L0_attn_b_Wq, L0_attn_b_Wk, L0_attn_b_Wv, L0_attn_b_Wpost)
    x = x + _L0_ffn_ref(_layernorm(x, axis=-1), L0_ffn_Wr, L0_ffn_Wg, L0_ffn_Wu, L0_ffn_Wd, L0_ffn_Sg, L0_ffn_Su, L0_ffn_Sd)
    return x

_drawn_inputs = setup_inputs


def setup_inputs(seed=0):
    import zlib

    import numpy as np

    out = dict(_drawn_inputs(seed))
    spreads = {}
    factors = {'L0_attn_a_w_q': 8.0,
     'L0_attn_a_w_k': 8.0,
     'L0_attn_b_Wq': 8.0,
     'L0_attn_b_Wk': 8.0,
     'L0_attn_b_Wv': 7.806,
     'L0_attn_b_Wpost': 7.317}
    for name, (base, spread) in spreads.items():
        noise = np.random.default_rng([zlib.crc32(name.encode()), seed]).standard_normal(out[name].shape)
        drawn = base * np.exp(spread * noise) if base else spread * noise
        out[name] = jnp.asarray(drawn.astype(out[name].dtype))
    for name, factor in factors.items():
        out[name] = (out[name] * factor).astype(out[name].dtype)
    return out
```

```python
from contextlib import ExitStack

import concourse.bass as bass
from concourse import mybir

F32 = mybir.dt.float32
F32R = mybir.dt.float32r
BF16 = mybir.dt.bfloat16
I32 = mybir.dt.int32
ALU = mybir.AluOpType
ACT = mybir.ActivationFunctionType
AX = mybir.AxisListType

P = 128
BATCH, SEQ = 16, 256
TILES = SEQ // P
HEADS, DH = 16, 64
PAIRS = HEADS // 2
EXPERTS = 16
EPS = 1e-5
SCALE = 1.0 / 8.0
NEG = -3.0e38

V_PARTS = 4
PROLOGUE_USES = 1 + V_PARTS + 3
USES = 1 + V_PARTS + HEADS + PAIRS + 2
LAYER_USES = BATCH * USES
END_USES = 3

FTOK = 512
FTILES = FTOK // P
FUNITS = BATCH * SEQ // FTOK
FPAIRS = EXPERTS // 2
FBLOCKS = FPAIRS + 1
FLAG = 3
MISC_USES = 4


class Unit:

    def __init__(self, it, c, first=False, last=False, end=False):
        self.it, self.c, self.first, self.last, self.end = it, c, first, last, end
        self.par = c % 2

    def count(self, per, plus):
        return self.it * (2 * per) + (per * self.c + plus)


def wait(eng, sem, value):
    if isinstance(value, int) and value <= 0:
        return
    eng.wait_ge(sem, value)


def each_unit(eng, units, body):
    body(Unit(0, 0, first=True))
    with eng.Fori(0, (units - 2) // 2) as it:
        body(Unit(it, 1))
        body(Unit(it, 2))
    body(Unit((units - 2) // 2, 1, last=True))


def attention_stream(first, last):
    out = []
    for h in range(HEADS):
        step = [("probs_t", h)]
        if h + 3 < HEADS or not last:
            step.append(("y", h + 3))
        pair_before = h % 2 == 0 and (h or not first)
        if pair_before:
            step.append(("rsum", h // 2 - 1))
        if h + 2 < HEADS or not last:
            step.append(("scores", h + 2))
        if pair_before:
            step.append(("av", h // 2 - 1))
        if not first and h == 12:
            step.append(("out", 0))
        if not first and h == 14:
            step.append(("out_t", 0))
        if not last and h == 8:
            step.append(("x_t", 0))
        if not last and 9 <= h < 9 + V_PARTS:
            step.append(("v", h - 9))
        out.append(step)
    return out


EPILOGUE = [("rsum", -1), ("av", -1), ("out", 0), ("out_t", 0)]
PROLOGUE = [("x_t", 0)] + [("v", i) for i in range(V_PARTS)] + [("y", 0), ("y", 1), ("scores", 0), ("y", 2), ("scores", 1)]
BANKED = ("x_t", "v", "y", "rsum", "out", "out_t")


def use_positions(events):
    out = {}
    for e in events:
        if e[0] in BANKED:
            out[e] = len(out)
    return out


def build_program(nc, x_in, wq_a, wk_a, wv_a, wo_a, wq_b, wk_b, wv_b, wo_b, wr, wg, wu, wd, sg, su, sd, out):
    ctx = ExitStack()
    with ctx:
        def sb(name, shape, dt=F32):
            return ctx.enter_context(nc.sbuf_tensor(name, shape, dt))

        def sem(name):
            return ctx.enter_context(nc.semaphore(name))

        x = sb("x", [P, BATCH * TILES, P])
        ident = sb("ident", [P, P])
        zero = sb("zero", [P, 1])
        ident_b = sb("ident_b", [P, P], BF16)
        causal = sb("causal", [P, P], BF16)
        select = sb("select", [3 * EXPERTS, FPAIRS, P], BF16)
        rank = sb("rank", [P, FTILES, EXPERTS])

        m_hi = sb("m_hi", [P, HEADS, P], F32R)
        m_lo = sb("m_lo", [P, HEADS, P], F32R)
        v_hi = sb("v_hi", [P, HEADS * DH], F32R)
        v_lo = sb("v_lo", [P, HEADS * DH], F32R)
        o_hi = sb("o_hi", [P, PAIRS, P], F32R)
        o_lo = sb("o_lo", [P, PAIRS, P], F32R)
        raw_b = sb("raw_b", [P, 4, HEADS * DH])

        g_hi = sb("g_hi", [P, FBLOCKS, P], F32R)
        g_lo = sb("g_lo", [P, FBLOCKS, P], F32R)
        u_hi = sb("u_hi", [P, FBLOCKS, P], F32R)
        u_lo = sb("u_lo", [P, FBLOCKS, P], F32R)
        d_hi = sb("d_hi", [P, FBLOCKS, P], F32R)
        d_lo = sb("d_lo", [P, FBLOCKS, P], F32R)
        r_hi = sb("r_hi", [P, EXPERTS], F32R)
        r_lo = sb("r_lo", [P, EXPERTS], F32R)
        raw_f = sb("raw_f", [P, 3, FBLOCKS, P])
        raw_r = sb("raw_r", [P, EXPERTS])

        xt_hi = sb("xt_hi", [P, 2, FTOK], F32R)
        xt_lo = sb("xt_lo", [P, 2, FTOK], F32R)
        wide = sb("wide", [P, 4, HEADS * DH])
        y_hi = sb("y_hi", [P, 2, SEQ], F32R)
        y_lo = sb("y_lo", [P, 2, SEQ], F32R)
        probs = sb("probs", [P, 2, TILES, SEQ])
        probs_t = sb("probs_t", [P, 4, TILES, SEQ])
        cat = sb("cat", [P, 2, PAIRS, SEQ])
        cat_hi = sb("cat_hi", [P, PAIRS, SEQ], F32R)
        cat_lo = sb("cat_lo", [P, PAIRS, SEQ], F32R)
        rsum = sb("rsum", [P, 2, SEQ])
        sums = sb("sums", [P, 2, HEADS, TILES])
        negmax = sb("negmax", [P, 2, HEADS, TILES])
        rec = sb("rec", [P, 2, TILES, 2])
        rec_wide = sb("rec_wide", [P, 2, TILES, 2, DH])
        out_s = sb("out_s", [P, SEQ])
        xn = sb("xn", [P, FTILES, P])
        stats = sb("stats", [P, FTILES, 6])
        moments = sb("moments", [P, 3, FTILES])
        var = sb("var", [P, FTILES])
        newton = sb("newton", [P, 3, FTILES])
        prob_r = sb("prob_r", [P, 4, FTILES, EXPERTS])
        top = sb("top", [P, 4, FTILES])
        cw_parts = sb("cw_parts", [P, FTILES, P // EXPERTS, EXPERTS], BF16)
        cw_t = sb("cw_t", [3 * EXPERTS, 2, FTOK], BF16)

        values = wide[:, :, :].rearrange("p (s t) n -> p s t n", s=2)
        flat = wide[:, :, :].rearrange("p a n -> p (a n)")
        silu = flat[:, 0:2 * FTOK].rearrange("p (r n) -> p r n", r=2)
        hid = flat[:, 2 * FTOK:5 * FTOK].rearrange("p (r n) -> p r n", r=3)
        fout_s = flat[:, 5 * FTOK:6 * FTOK]
        hid_hi = cat_hi[:, :, :].rearrange("p a n -> p (a n)")[:, 0:3 * FTOK].rearrange("p (r n) -> p r n", r=3)
        hid_lo = cat_lo[:, :, :].rearrange("p a n -> p (a n)")[:, 0:3 * FTOK].rearrange("p (r n) -> p r n", r=3)

        banks = [ctx.enter_context(nc.psum_tensor(f"bank{i}", [P, 512], F32)) for i in range(8)]
        proj, score, turn, heads_out = banks[0:2], banks[2:4], banks[4:6], banks[6:8]
        gate, up, spread, misc, acc = banks[0:2], banks[2:4], banks[4], banks[5], banks[6:8]
        misc_b = misc[:, :].bitcast(BF16)

        loaded_x = sem("loaded_x")
        loaded_a = sem("loaded_a")
        loaded_b = sem("loaded_b")
        loaded_f = sem("loaded_f")
        stored = sem("stored")
        consts = sem("consts")
        prep_made = sem("prep_made")
        prep_hi = sem("prep_hi")
        prep_lo = sem("prep_lo")
        prep_turned = sem("prep_turned")
        dve_chain = sem("dve_chain")

        proj_made = sem("proj_made")
        proj_free = [sem("proj_free0"), sem("proj_free1")]
        score_made = sem("score_made")
        turn_made = sem("turn_made")
        heads_made = sem("heads_made")
        xt_hi_done = sem("xt_hi_done")
        y_hi_done = sem("y_hi_done")
        exp_done = sem("exp_done")
        gelu_done = sem("gelu_done")
        xn_done = sem("xn_done")
        max_done = sem("max_done")
        turn_done = sem("turn_done")
        rec_small = sem("rec_small")
        rec_done = sem("rec_done")
        norm_done = sem("norm_done")
        cat_hi_done = sem("cat_hi_done")
        cat_lo_done = sem("cat_lo_done")

        gate_made = sem("gate_made")
        up_made = sem("up_made")
        spread_made = sem("spread_made")
        down_made = sem("down_made")
        misc_made = sem("misc_made")
        misc_free = sem("misc_free")
        fxt_hi_done = sem("fxt_hi_done")
        silu_done = sem("silu_done")
        hid_hi_done = sem("hid_hi_done")
        router_exp = sem("router_exp")
        fout_done = sem("fout_done")
        fxn_done = sem("fxn_done")
        gated = sem("gated")
        weighted = sem("weighted")
        cw_done = sem("cw_done")
        hid_lo_done = sem("hid_lo_done")

        block = ctx.enter_context(nc.Block())

        def use(layer, unit, pos):
            if unit is None:
                m, turns = LAYER_USES * layer + pos, 0
            elif unit.first:
                m, turns = LAYER_USES * layer + PROLOGUE_USES + pos, 0
            else:
                m, turns = LAYER_USES * layer + PROLOGUE_USES - END_USES + USES * unit.c + pos, unit.it * USES
            return m % 2, m // 2 + turns, m + turns * 2

        def mark(layer, unit, pos):
            bank, before, m = use(layer, unit, pos)
            return bank, before + 1, m + 1

        POS = {(f, l): use_positions([e for s in attention_stream(f, l) for e in s])
               for f, l in ((True, False), (False, False), (False, True))}
        POS_PRO = use_positions(PROLOGUE)
        POS_EPI = use_positions(EPILOGUE)

        def pos_of(unit, event):
            return POS[(unit.first, unit.last)][event]

        def mark_of(layer, unit, event):
            if unit is None:
                return mark(layer, None, POS_PRO[event])
            if unit.end:
                m = LAYER_USES * (layer + 1) - END_USES + POS_EPI[event]
                return m % 2, m // 2 + 1, m + 1
            return mark(layer, unit, pos_of(unit, event))

        def y_mark(layer, unit, h):
            if h > 2:
                return mark_of(layer, unit, ("y", h))
            if unit.first:
                return mark_of(layer, None, ("y", h))
            return mark(layer, unit, -1)

        def before_layer(eng, layer):
            if layer >= 0:
                bank, frees, _ = mark_of(layer, END, ("out_t", 0))
                eng.wait_ge(proj_free[bank], frees)

        END = Unit(BATCH // 2, 0, end=True)
        FEND = Unit(FUNITS // 2, 0, end=True)
        FL = FUNITS * MISC_USES

        def misc_use(layer, unit, what):
            if unit is None:
                return FL * layer + ("x", "logits", "cw").index(what)
            if unit.end:
                return FL * (layer + 1) - 1
            if unit.first:
                return FL * layer + 3 + ("x", "logits", "cw").index(what)
            order = ("out",) if unit.last else ("x", "logits", "out", "cw")
            return unit.count(MISC_USES, FL * layer + 2 + order.index(what))

        def before_ffn_end(eng, layer):
            eng.wait_ge(misc_free, FL * (layer + 1))

        raw_a = wide

        def attention_jobs(layer):
            jobs = []
            if layer == 0:
                q_rows, k_rows = raw_a[:, 0, :], raw_a[:, 1, :]
                for c in range(2):
                    jobs.append((("turn", [raw_a[:, 2, (4 * c + j) * P:(4 * c + j + 1) * P] for j in range(4)]), None, 1.0,
                                 v_hi[:, c * 512:(c + 1) * 512], v_lo[:, c * 512:(c + 1) * 512]))
                for c in range(2):
                    jobs.append((("turn", [raw_a[:, 3, (4 * c + j) * P:(4 * c + j + 1) * P] for j in range(4)]), None, 1.0,
                                 o_hi[:, 4 * c:4 * c + 4, :].rearrange("p a n -> p (a n)"),
                                 o_lo[:, 4 * c:4 * c + 4, :].rearrange("p a n -> p (a n)")))
            else:
                q_rows, k_rows = wide[:, 0, :], wide[:, 1, :]
                for c in range(2):
                    jobs.append((None, raw_b[:, 2, c * 512:(c + 1) * 512], 1.0,
                                 v_hi[:, c * 512:(c + 1) * 512], v_lo[:, c * 512:(c + 1) * 512]))
                for c in range(2):
                    jobs.append((None, raw_b[:, 3, c * 512:(c + 1) * 512], 1.0,
                                 o_hi[:, 4 * c:4 * c + 4, :].rearrange("p a n -> p (a n)"),
                                 o_lo[:, 4 * c:4 * c + 4, :].rearrange("p a n -> p (a n)")))
            for c in range(4):
                heads = [8 * (c // 2) + 2 * j + c % 2 for j in range(4)]
                pairs = [(q_rows[DH * (h % 2):DH * (h % 2) + DH, (h // 2) * P:(h // 2 + 1) * P],
                          k_rows[DH * (h % 2):DH * (h % 2) + DH, (h // 2) * P:(h // 2 + 1) * P]) for h in heads]
                jobs.append((("product", pairs), None, SCALE,
                             m_hi[:, heads[0]:heads[-1] + 1:2, :], m_lo[:, heads[0]:heads[-1] + 1:2, :]))
            return jobs

        def ffn_jobs():
            jobs = []
            for w, (hi, lo) in enumerate(((g_hi, g_lo), (u_hi, u_lo), (d_hi, d_lo))):
                for a, b in ((0, 4), (4, 8), (8, 9)):
                    jobs.append((None, raw_f[:, w, a:b, :].rearrange("p a n -> p (a n)"), 1.0,
                                 hi[:, a:b, :].rearrange("p a n -> p (a n)"), lo[:, a:b, :].rearrange("p a n -> p (a n)")))
            jobs.append((None, raw_r[:, :], 1.0, r_hi[:, :], r_lo[:, :]))
            return jobs

        JOBS = [attention_jobs(0), ffn_jobs(), attention_jobs(1)]
        JOB_START = [0, len(JOBS[0]), len(JOBS[0]) + len(JOBS[1])]
        MADE_START = [0, len(JOBS[0]), len(JOBS[0])]

        def prep_pe(eng, stage):
            made = MADE_START[stage]
            for i, (work, _, _, hi, _) in enumerate(JOBS[stage]):
                if work is None:
                    continue
                bank = banks[i % 4]
                if i >= 4 and JOBS[stage][i - 4][0] is not None:
                    eng.wait_ge(prep_lo, JOB_START[stage] + i - 3)
                for j, piece in enumerate(work[1]):
                    dst = bank[:, j * P:(j + 1) * P]
                    if work[0] == "turn":
                        last = eng.transpose(dst, piece, ident[:, :])
                    else:
                        last = eng.matmul(dst, piece[0], piece[1], start=True, stop=True)
                made += 1
                last.then_inc(prep_made, 1)

        def job_source(stage, i):
            work, src, _, hi, _ = JOBS[stage][i]
            if work is None:
                return src
            if work[0] == "product":
                return banks[i % 4][:, :].rearrange("p (a n) -> p a n", a=4)
            return banks[i % 4][:, :]

        def prep_act(eng, stage):
            made = MADE_START[stage]
            for i, (work, _, scale, hi, _) in enumerate(JOBS[stage]):
                if work is not None:
                    made += 1
                    eng.wait_ge(prep_made, made)
                eng.activation(hi, job_source(stage, i), ACT.Copy, scale=scale).then_inc(prep_hi, 1)

        def prep_dve(eng, stage):
            for i, (work, _, scale, hi, lo) in enumerate(JOBS[stage]):
                eng.wait_ge(prep_hi, JOB_START[stage] + i + 1)
                eng.scalar_tensor_tensor(out=lo, in0=job_source(stage, i), scalar=scale, in1=hi.bitcast(F32),
                                         op0=ALU.mult, op1=ALU.subtract).then_inc(prep_lo, 1)

        def prepared(eng, stage):
            eng.wait_ge(prep_lo, JOB_START[stage] + len(JOBS[stage]))

        def turn_raw_pe(eng):
            eng.wait_ge(loaded_b, 4 * 16)
            for c in range(4):
                for j in range(4):
                    last = eng.transpose(banks[4 + c][:, j * P:(j + 1) * P],
                                         raw_b[:, c // 2, ((c % 2) * 4 + j) * P:((c % 2) * 4 + j + 1) * P], ident[:, :])
                last.then_inc(prep_turned, 1)
            eng.wait_ge(prep_turned, 8)

        def turn_raw_act(eng):
            eng.wait_ge(loaded_b, 4 * 16)
            for c in range(4):
                eng.wait_ge(prep_turned, 4)
                eng.activation(wide[:, c // 2, (c % 2) * 512:(c % 2 + 1) * 512], banks[4 + c][:, :], ACT.Copy)\
                   .then_inc(prep_turned, 1)

        @block.sync
        def _(eng):
            x_tiles = x_in.rearrange("b (t p) d -> p (b t) d", p=P)
            eng.dma_start(raw_a[:, 0, :].rearrange("p (j d) -> p j d", d=P), wq_a.rearrange("(j g) q d -> (g q) j d", g=2)).then_inc(loaded_a, 16)
            eng.dma_start(raw_a[:, 1, :].rearrange("p (j d) -> p j d", d=P), wk_a.rearrange("(j g) q d -> (g q) j d", g=2)).then_inc(loaded_a, 16)
            eng.dma_start(x[:, 0:8, :], x_tiles[:, 0:8, :]).then_inc(loaded_x, 16)
            eng.dma_start(x[:, 8:32, :], x_tiles[:, 8:32, :]).then_inc(loaded_x, 16)
            eng.dma_start(raw_f[:, 0, 0:FPAIRS, :].rearrange("p a (g f) -> p (a g) f", g=2), wg.rearrange("e d f -> d e f")).then_inc(loaded_f, 16)
            eng.dma_start(raw_f[:, 1, 0:FPAIRS, :].rearrange("p a (g f) -> p (a g) f", g=2), wu.rearrange("e d f -> d e f")).then_inc(loaded_f, 16)
            eng.dma_start(raw_f[:, 2, 0:FPAIRS, :], wd.rearrange("(a g) f d -> (g f) a d", g=2)).then_inc(loaded_f, 16)
            for w, part in enumerate((sg, su, sd)):
                eng.dma_start(raw_f[:, w, FPAIRS, :], part).then_inc(loaded_f, 16)
            eng.dma_start(raw_r[:, :], wr).then_inc(loaded_f, 16)
            for w, part in enumerate((wq_b, wk_b, wv_b)):
                eng.dma_start(raw_b[:, w, :], part).then_inc(loaded_b, 16)
            eng.dma_start(raw_b[:, 3, :].rearrange("p (j n) -> p j n", n=P), wo_b.rearrange("(j p) n -> p j n", p=P)).then_inc(loaded_b, 16)

            o_tiles = out.rearrange("b (t p) d -> p (b t) d", p=P)
            for w in range(FUNITS):
                done = FL + 2 + MISC_USES * (w + 1) + (3 if w < FUNITS - 2 else 1) if w < FUNITS - 1 else 2 * FL
                eng.wait_ge(misc_free, done)
                eng.dma_start(o_tiles[:, FTILES * w:FTILES * (w + 1), :], x[:, FTILES * w:FTILES * (w + 1), :]).then_inc(stored, 16)
            eng.wait_ge(stored, 16 * FUNITS)

        @block.gpsimd
        def _(eng):
            eng.memset(ident[:, :], 0.0).then_inc(consts, 1)
            eng.memset(ident_b[:, :], 0.0).then_inc(consts, 1)
            eng.memset(zero[:, :], 0.0).then_inc(consts, 1)
            eng.memset(causal[:, :], 0.0).then_inc(consts, 1)
            eng.memset(select[:, :, :], 0.0).then_inc(consts, 1)
            eng.memset(cw_parts[:, :, :, :], 0.0).then_inc(consts, 1)
            eng.wait_ge(consts, 6)
            for m in (ident, ident_b):
                eng.affine_select(out=m[:, :], in_=m[:, :], compare_op=ALU.not_equal, fill=1.0, base=0,
                                  pattern=[[-1, P]], channel_multiplier=1).then_inc(consts, 1)
            eng.affine_select(out=causal[:, :], in_=causal[:, :], compare_op=ALU.is_ge, fill=NEG, base=0,
                              pattern=[[-1, P]], channel_multiplier=1).then_inc(consts, 1)
            for e in range(EXPERTS):
                eng.memset(rank[:, :, e:e + 1], float(EXPERTS - e)).then_inc(consts, 1)
            for part in range(3):
                view = select[:, :, :].rearrange("p a (g f) -> p a g f", g=2)
                eng.affine_select(out=view, in_=view, compare_op=ALU.not_equal, fill=1.0, base=-EXPERTS * part,
                                  pattern=[[-2, FPAIRS], [-1, 2], [0, DH]], channel_multiplier=1).then_inc(consts, 1)
                eng.wait_ge(consts, 9 + EXPERTS + part + 1)

            def split(layer, unit, c, wait_out):
                b = unit.count(PAIRS, BATCH * PAIRS * layer + c - PAIRS)
                slot = 1 - unit.par
                if layer == 0:
                    eng.wait_ge(norm_done, b + 1)
                else:
                    eng.wait_ge(gelu_done, unit.count(2, -2 + c // 4 + 1))
                if wait_out is not None:
                    eng.wait_ge(proj_made, wait_out)
                eng.tensor_tensor(cat_hi[:, c, :], cat[:, slot, c, :], zero[:, :].to_broadcast([P, SEQ]), ALU.subtract).then_inc(cat_hi_done, 1)
                eng.wait_ge(cat_hi_done, b + 1)
                eng.tensor_tensor(cat_lo[:, c, :], cat[:, slot, c, :], cat_hi[:, c, :].bitcast(F32), ALU.subtract)\
                   .then_inc(cat_lo_done, 1)

            def pool_attention(layer):
                def unit_work(unit):
                    for p in range(PAIRS):
                        if not unit.first and 1 <= p <= 4:
                            for c in (2 * p - 2, 2 * p - 1):
                                out_before = None
                                if c == 0:
                                    pos = POS[(False, False)][("out", 0)] - USES
                                    out_before = mark(layer, unit, pos)[2]
                                    if isinstance(unit.it, int) and 2 * unit.it + unit.c < 2:
                                        out_before = None
                                split(layer, unit, c, out_before)
                each_unit(eng, BATCH, unit_work)
                for c in range(PAIRS):
                    last = Unit(BATCH // 2 - 1, 1, last=True)
                    split(layer, END, c, mark_of(layer, last, ("out", 0))[2] if c == 0 else None)

            def pool_ffn(layer):
                def unit_work(unit):
                    for f in range(FBLOCKS):
                        k = unit.count(FBLOCKS, FUNITS * FBLOCKS * layer + f)
                        slot = (unit.par * FBLOCKS + f) % 3
                        eng.wait_ge(hid_hi_done, k + 1)
                        eng.tensor_tensor(hid_lo[:, slot, :], hid[:, slot, :], hid_hi[:, slot, :].bitcast(F32), ALU.subtract)\
                           .then_inc(hid_lo_done, 1)
                each_unit(eng, FUNITS, unit_work)

            pool_attention(0)
            pool_ffn(0)
            pool_attention(1)
            pool_ffn(1)

        @block.scalar
        def _(eng):
            eng.dma_start(raw_a[:, 2, :].rearrange("p (j d) -> p j d", d=P), wv_a.rearrange("(j g) v d -> (g v) j d", g=2)).then_inc(loaded_a, 16)
            eng.dma_start(raw_a[:, 3, :], wo_a).then_inc(loaded_a, 16)

            def take_x(layer, unit, number, xt_slot):
                bank, _, made = mark_of(layer, unit, ("x_t", 0))
                eng.wait_ge(proj_made, made)
                eng.activation(xt_hi[:, xt_slot, 0:SEQ], proj[bank][:, 0:SEQ], ACT.Copy).then_inc(xt_hi_done, 1)

            def take_v(layer, unit, i, slot):
                bank, _, made = mark_of(layer, unit, ("v", i))
                eng.wait_ge(proj_made, made)
                eng.activation(values[:, slot, i // 2, (i % 2) * 512:(i % 2 + 1) * 512], proj[bank][:, :], ACT.Copy)\
                   .then_inc(proj_free[bank], 1)

            def take_y(layer, unit, h):
                bank, _, made = mark_of(layer, unit, ("y", h))
                eng.wait_ge(proj_made, made)
                eng.activation(y_hi[:, h % 2, :], proj[bank][:, 0:SEQ], ACT.Copy).then_inc(y_hi_done, 1)

            def exps(layer, unit, h):
                n = unit.count(HEADS, BATCH * HEADS * layer + h)
                slot = (unit.par + h // HEADS) % 2
                hh = h % HEADS
                eng.wait_ge(max_done, n + 1)
                for t in range(TILES):
                    keys = SEQ if layer else (t + 1) * P
                    last = eng.activation(probs[:, h % 2, t, 0:keys], score[h % 2][:, t * SEQ:t * SEQ + keys], ACT.Exp,
                                          bias=negmax[:, slot, hh, t:t + 1], accum_out=sums[:, slot, hh, t:t + 1])
                last.then_inc(exp_done, 1)

            def take_rsum(layer, unit, p):
                bank, _, made = mark_of(layer, unit, ("rsum", p))
                eng.wait_ge(proj_made, made)
                wait(eng, norm_done, unit.count(PAIRS, BATCH * PAIRS * layer + p - 1))
                eng.activation(rsum[:, p % 2, :], proj[bank][:, 0:SEQ], ACT.Copy).then_inc(proj_free[bank], 1)

            def gelu(unit):
                slot = 1 - unit.par
                eng.wait_ge(norm_done, unit.count(PAIRS, BATCH * PAIRS))
                for half in range(2):
                    part = cat[:, slot, 4 * half:4 * half + 4, :]
                    eng.activation(part, part, ACT.Gelu).then_inc(gelu_done, 1)

            def take_out(layer, unit):
                bank, _, made = mark_of(layer, unit, ("out", 0))
                eng.wait_ge(proj_made, made)
                eng.activation(out_s[:, :], proj[bank][:, 0:SEQ], ACT.Copy).then_inc(proj_free[bank], 1)

            def act_attention(layer):
                start = Unit(0, 0, first=True)
                take_x(layer, None, 0, 0)
                take_v(layer, None, 0, 0)
                take_v(layer, None, 2, 0)
                take_y(layer, None, 0)
                take_y(layer, None, 1)
                exps(layer, start, 0)
                take_y(layer, None, 2)
                exps(layer, start, 1)

                def unit_work(unit):
                    for h, step in enumerate(attention_stream(unit.first, unit.last)):
                        if ("y", h + 3) in step:
                            take_y(layer, unit, h + 3)
                        if ("rsum", h // 2 - 1) in step:
                            take_rsum(layer, unit, h // 2 - 1)
                        if ("scores", h + 2) in step:
                            exps(layer, unit, h + 2)
                        if layer and not unit.first and h == 1:
                            gelu(unit)
                        if ("out", 0) in step:
                            take_out(layer, unit)
                        if ("x_t", 0) in step:
                            take_x(layer, unit, 1, 1 - unit.par)
                        for i in (0, 2):
                            if ("v", i) in step:
                                take_v(layer, unit, i, 1 - unit.par)
                each_unit(eng, BATCH, unit_work)
                take_rsum(layer, END, -1)
                if layer:
                    gelu(END)
                take_out(layer, END)

            def act_ffn(layer):
                def take_fx(unit, slot):
                    eng.wait_ge(misc_made, misc_use(layer, unit, "x") + 1)
                    eng.activation(xt_hi[:, slot, :], misc[:, :], ACT.Copy).then_inc(fxt_hi_done, 1)

                def router(unit):
                    eng.wait_ge(misc_free, misc_use(layer, unit, "logits") + 1)
                    eng.activation(prob_r[:, 1, :, :], prob_r[:, 0, :, :], ACT.Exp).then_inc(router_exp, 1)

                def take_cw(unit, slot):
                    use_no = misc_use(layer, unit, "cw")
                    eng.wait_ge(misc_made, use_no + 1)
                    eng.activation(cw_t[:, slot, :], misc_b[0:3 * EXPERTS, 0:FTOK], ACT.Copy).then_inc(misc_free, 1)

                def silus(unit, f):
                    k = unit.count(FBLOCKS, FUNITS * FBLOCKS * layer + f)
                    slot = (unit.par * FBLOCKS + f) % 2
                    eng.wait_ge(gate_made, k + 1)
                    wait(eng, gated, k - 1)
                    eng.activation(silu[:, slot, :], gate[slot][:, :], ACT.Silu).then_inc(silu_done, 1)

                def high(unit, f):
                    k = unit.count(FBLOCKS, FUNITS * FBLOCKS * layer + f)
                    slot = (unit.par * FBLOCKS + f) % 3
                    if f == FBLOCKS - 1:
                        eng.wait_ge(gated, k + 1)
                    else:
                        eng.wait_ge(weighted, unit.count(FPAIRS, FUNITS * FPAIRS * layer + f) + 1)
                    wait(eng, down_made, k - 2)
                    eng.activation(hid_hi[:, slot, :], hid[:, slot, :], ACT.Copy).then_inc(hid_hi_done, 1)

                def take_fout(unit):
                    slot = 1 - unit.par
                    eng.wait_ge(down_made, unit.count(FBLOCKS, FUNITS * FBLOCKS * layer))
                    eng.activation(fout_s, acc[slot][:, :], ACT.Copy).then_inc(fout_done, 1)

                take_fx(None, 0)
                router(None)
                take_cw(None, 0)

                def unit_work(unit):
                    for f in range(FBLOCKS):
                        silus(unit, f)
                        if f:
                            high(unit, f - 1)
                        if f == 3 and not unit.first:
                            take_fout(unit)
                        if not unit.last:
                            if f == 2:
                                take_fx(unit, 1 - unit.par)
                            if f == 4:
                                router(unit)
                    high(unit, FBLOCKS - 1)
                    if not unit.last:
                        take_cw(unit, 1 - unit.par)
                each_unit(eng, FUNITS, unit_work)
                take_fout(FEND)

            eng.wait_ge(loaded_a, 4 * 16)
            prep_act(eng, 0)
            act_attention(0)
            before_layer(eng, 0)
            eng.wait_ge(loaded_f, 7 * 16)
            prep_act(eng, 1)
            act_ffn(0)
            before_ffn_end(eng, 0)
            turn_raw_act(eng)
            prep_act(eng, 2)
            act_attention(1)
            before_layer(eng, 1)
            act_ffn(1)

        @block.tensor
        def _(eng):
            def claim(layer, unit, event):
                bank, frees, _ = mark_of(layer, unit, event)
                wait(eng, proj_free[bank], frees - 1)
                return proj[bank]

            def three(dst, a_hi, a_lo, b_hi, b_lo, start=True, stop=True, masked=None):
                eng.matmul(dst, a_hi, b_hi, start=start, stop=False)
                if masked is not None:
                    eng.matmul(masked, ident_b[:, :], causal[:, :], start=False, stop=False, skip_group_check=True)
                eng.matmul(dst, a_hi, b_lo, start=False, stop=False)
                return eng.matmul(dst, a_lo, b_hi, start=False, stop=stop)

            def attention(layer):
                def x_t(unit, slot, number):
                    bank = claim(layer, unit, ("x_t", 0))
                    eng.wait_ge(xn_done, number)
                    for t in range(TILES):
                        last = eng.transpose(bank[:, t * P:(t + 1) * P], xn[:, t, :], ident[:, :])
                    last.then_inc(proj_made, 1)

                def v(unit, i, slot):
                    bank = claim(layer, unit, ("v", i))
                    if i == 0:
                        b, frees, _ = mark_of(layer, unit, ("x_t", 0))
                        eng.wait_ge(proj_free[b], frees)
                    tok = slice((i // 2) * P, (i // 2 + 1) * P)
                    cols = slice((i % 2) * 512, (i % 2 + 1) * 512)
                    three(bank[:, :], xt_hi[:, slot, tok], xt_lo[:, slot, tok], v_hi[:, cols], v_lo[:, cols])\
                        .then_inc(proj_made, 1)

                def y(unit, h, slot):
                    bank = claim(layer, unit, ("y", h))
                    three(bank[:, 0:SEQ], m_hi[:, h % HEADS, :], m_lo[:, h % HEADS, :],
                          xt_hi[:, slot, 0:SEQ], xt_lo[:, slot, 0:SEQ]).then_inc(proj_made, 1)

                def scores(mark_y, h, slot):
                    b, frees, _ = mark_y
                    eng.wait_ge(proj_free[b], frees)
                    for t in range(TILES):
                        keys = SEQ if layer else (t + 1) * P
                        dst = score[h % 2][:, t * SEQ:t * SEQ + keys]
                        q = slice(t * P, (t + 1) * P)
                        diagonal = None if layer else score[h % 2][:, t * SEQ + t * P:t * SEQ + (t + 1) * P]
                        last = three(dst, y_hi[:, h % 2, q], y_lo[:, h % 2, q], xt_hi[:, slot, 0:keys], xt_lo[:, slot, 0:keys],
                                     masked=diagonal)
                    last.then_inc(score_made, 1)

                def probs_turned(unit, h):
                    n = unit.count(HEADS, BATCH * HEADS * layer + h)
                    eng.wait_ge(exp_done, n + 1)
                    wait(eng, turn_done, n - 1)
                    for k in range(TILES):
                        for q in range(TILES):
                            if layer or k <= q:
                                last = eng.transpose(turn[h % 2][:, k * SEQ + q * P:k * SEQ + (q + 1) * P],
                                                     probs[:, h % 2, q, k * P:(k + 1) * P], ident[:, :])
                    last.then_inc(turn_made, 1)

                def rsums(unit, p):
                    g = unit.count(PAIRS, BATCH * PAIRS * layer + p)
                    bank = claim(layer, unit, ("rsum", p))
                    eng.wait_ge(rec_done, g + 1)
                    for t in range(TILES):
                        last = eng.transpose(bank[:, t * P:(t + 1) * P],
                                             rec_wide[:, p % 2, t, :, :].rearrange("p a n -> p (a n)"), ident[:, :])
                    last.then_inc(proj_made, 1)

                def av(unit, p):
                    eng.wait_ge(turn_done, unit.count(HEADS, BATCH * HEADS * layer + 2 * p + 2))
                    slot = unit.par if p >= 0 else 1 - unit.par
                    for k in range(TILES):
                        q0 = 0 if layer else k * P
                        for g in range(2):
                            h = (2 * p + g) % HEADS
                            last = eng.matmul(heads_out[p % 2][DH * g:DH * g + DH, q0:SEQ],
                                              values[:, slot, k, h * DH:(h + 1) * DH],
                                              probs_t[:, h % 4, k, q0:SEQ], start=(k == 0), stop=(k == TILES - 1),
                                              skip_group_check=True)
                    last.then_inc(heads_made, 1)

                def out(unit, b):
                    bank = claim(layer, unit, ("out", 0))
                    eng.wait_ge(cat_lo_done, b)
                    for j in range(PAIRS):
                        last = three(bank[:, 0:SEQ], o_hi[:, j, :], o_lo[:, j, :], cat_hi[:, j, :], cat_lo[:, j, :],
                                     start=(j == 0), stop=(j == PAIRS - 1))
                    last.then_inc(proj_made, 1)

                def out_t(unit):
                    bank = claim(layer, unit, ("out_t", 0))
                    b, frees, _ = mark_of(layer, unit, ("out", 0))
                    eng.wait_ge(proj_free[b], frees)
                    for t in range(TILES):
                        last = eng.transpose(bank[:, t * P:(t + 1) * P], out_s[:, t * P:(t + 1) * P], ident[:, :])
                    last.then_inc(proj_made, 1)

                start = Unit(0, 0, first=True)
                for e, i in PROLOGUE:
                    if e == "x_t":
                        x_t(None, 0, BATCH * layer + 1)
                    elif e == "v":
                        v(None, i, 0)
                    elif e == "y":
                        y(None, i, 0)
                    else:
                        scores(mark_of(layer, None, ("y", i)), i, 0)

                def unit_work(unit):
                    for step in attention_stream(unit.first, unit.last):
                        for e, i in step:
                            if e == "probs_t":
                                probs_turned(unit, i)
                            elif e == "y":
                                y(unit, i, (unit.par + i // HEADS) % 2)
                            elif e == "scores":
                                scores(y_mark(layer, unit, i), i, (unit.par + i // HEADS) % 2)
                            elif e == "rsum":
                                rsums(unit, i)
                            elif e == "av":
                                av(unit, i)
                            elif e == "out":
                                out(unit, unit.count(PAIRS, BATCH * PAIRS * layer))
                            elif e == "out_t":
                                out_t(unit)
                            elif e == "x_t":
                                x_t(unit, 1 - unit.par, unit.count(1, BATCH * layer + 2))
                            else:
                                v(unit, i, 1 - unit.par)
                each_unit(eng, BATCH, unit_work)
                rsums(END, -1)
                av(END, -1)
                out(END, BATCH * PAIRS * (layer + 1))
                out_t(END)

            def ffn(layer):
                def x_t(unit, number):
                    no = misc_use(layer, unit, "x")
                    wait(eng, misc_free, no)
                    eng.wait_ge(fxn_done, number)
                    for t in range(FTILES):
                        last = eng.transpose(misc[:, t * P:(t + 1) * P], xn[:, t, :], ident[:, :])
                    last.then_inc(misc_made, 1)

                def logits(unit, slot):
                    no = misc_use(layer, unit, "logits")
                    eng.wait_ge(misc_free, no)
                    for t in range(FTILES):
                        tok = slice(t * P, (t + 1) * P)
                        last = three(misc[:, t * EXPERTS:(t + 1) * EXPERTS], xt_hi[:, slot, tok], xt_lo[:, slot, tok],
                                     r_hi[:, :], r_lo[:, :])
                    last.then_inc(misc_made, 1)

                def cw_turned(unit, number):
                    no = misc_use(layer, unit, "cw")
                    eng.wait_ge(misc_free, no)
                    eng.wait_ge(cw_done, number)
                    for t in range(FTILES):
                        last = eng.transpose(misc_b[:, t * P:(t + 1) * P],
                                             cw_parts[:, t, :, :].rearrange("p a e -> p (a e)"), ident_b[:, :])
                    last.then_inc(misc_made, 1)

                def blocks(unit, f):
                    k = unit.count(FBLOCKS, FUNITS * FBLOCKS * layer + f)
                    b = (unit.par * FBLOCKS + f) % 2
                    xs = xt_hi[:, unit.par, :], xt_lo[:, unit.par, :]
                    wait(eng, silu_done, k - 1)
                    three(gate[b][:, :], g_hi[:, f, :], g_lo[:, f, :], *xs).then_inc(gate_made, 1)
                    wait(eng, gated, k - 1)
                    three(up[b][:, :], u_hi[:, f, :], u_lo[:, f, :], *xs).then_inc(up_made, 1)
                    if f < FPAIRS:
                        wait(eng, weighted, unit.count(FPAIRS, FUNITS * FPAIRS * layer + f))
                        eng.matmul(spread[:, :], select[:, f, :], cw_t[:, unit.par, :], start=True, stop=True)\
                           .then_inc(spread_made, 1)

                def down(unit, f):
                    k = unit.count(FBLOCKS, FUNITS * FBLOCKS * layer + f)
                    slot = (unit.par * FBLOCKS + f) % 3
                    a = unit.par if f >= 0 else 1 - unit.par
                    f %= FBLOCKS
                    eng.wait_ge(hid_lo_done, k + 1)
                    three(acc[a][:, :], d_hi[:, f, :], d_lo[:, f, :], hid_hi[:, slot, :], hid_lo[:, slot, :],
                          start=(f == 0), stop=(f == FBLOCKS - 1)).then_inc(down_made, 1)

                def out_t(unit, number):
                    no = misc_use(layer, unit, "out")
                    eng.wait_ge(misc_free, no)
                    eng.wait_ge(fout_done, number)
                    for t in range(FTILES):
                        last = eng.transpose(misc[:, t * P:(t + 1) * P], fout_s[:, t * P:(t + 1) * P], ident[:, :])
                    last.then_inc(misc_made, 1)

                x_t(None, FUNITS * layer + 1)
                logits(None, 0)
                cw_turned(None, FUNITS * layer + 1)

                def unit_work(unit):
                    for f in range(FBLOCKS):
                        if f == 0:
                            eng.wait_ge(misc_free, FL * layer + 3 if unit.first else unit.count(MISC_USES, FL * layer + 2))
                        blocks(unit, f)
                        if f >= FLAG or not unit.first:
                            down(unit, f - FLAG)
                        if not unit.last:
                            if f == 2:
                                x_t(unit, unit.count(1, FUNITS * layer + 2))
                            if f == 3:
                                logits(unit, 1 - unit.par)
                        if f == 4 and not unit.first:
                            out_t(unit, unit.count(1, FUNITS * layer))
                        if not unit.last:
                            if f == 8:
                                cw_turned(unit, unit.count(1, FUNITS * layer + 2))
                each_unit(eng, FUNITS, unit_work)
                for f in range(FLAG):
                    down(FEND, f - FLAG)
                out_t(FEND, FUNITS * (layer + 1))

            eng.wait_ge(consts, 12 + EXPERTS)
            eng.wait_ge(loaded_a, 4 * 16)
            prep_pe(eng, 0)
            prepared(eng, 0)
            attention(0)
            before_layer(eng, 0)
            prepared(eng, 1)
            ffn(0)
            before_ffn_end(eng, 0)
            turn_raw_pe(eng)
            prep_pe(eng, 2)
            prepared(eng, 2)
            attention(1)
            before_layer(eng, 1)
            ffn(1)

        @block.vector
        def _(eng):
            class Chain:

                def __init__(self):
                    self.base, self.k = 0, 0

                def at(self, value):
                    self.base, self.k = value, 0

                def link(self, ins):
                    ins.then_inc(dve_chain, 1)
                    self.k += 1
                    eng.wait_ge(dve_chain, self.base + self.k)

            chain = Chain()
            def tiles_of(unit, ahead, tiles):
                if unit is None:
                    return x[:, 0:tiles, :]
                at = unit.count(tiles, ahead * tiles)
                return x[:, at:at + tiles, :] if isinstance(at, int) else x[:, bass.ds(at, tiles), :]

            def normalise(src, tiles, done):
                for t in range(tiles):
                    last = eng.bn_stats(stats[:, t, :], src[:, t, :])
                chain.link(last)
                even, odd = stats[:, 0:tiles, 1], stats[:, 0:tiles, 4]
                mean, diff, both = (moments[:, i, 0:tiles] for i in range(3))
                eng.tensor_tensor(mean, even, odd, ALU.add)
                eng.tensor_tensor(diff, even, odd, ALU.subtract)
                chain.link(eng.tensor_tensor(both, stats[:, 0:tiles, 2], stats[:, 0:tiles, 5], ALU.add))
                eng.tensor_scalar(mean, mean, 0.5, None, ALU.mult)
                chain.link(eng.scalar_tensor_tensor(out=diff, in0=diff, scalar=0.25, in1=diff, op0=ALU.mult, op1=ALU.mult))
                chain.link(eng.scalar_tensor_tensor(out=both, in0=both, scalar=1.0 / P, in1=diff, op0=ALU.mult, op1=ALU.add))
                v, r, a, b = var[:, 0:tiles], newton[:, 0, 0:tiles], newton[:, 1, 0:tiles], newton[:, 2, 0:tiles]
                chain.link(eng.tensor_scalar(v, both, EPS, None, ALU.add))
                chain.link(eng.tensor_scalar(a.bitcast(I32), v.bitcast(I32), 1, None, ALU.logical_shift_right))
                chain.link(eng.tensor_scalar(r.bitcast(I32), a.bitcast(I32), -1.0, float(0x5F3759DF), ALU.mult, ALU.add))
                for _ in range(3):
                    chain.link(eng.scalar_tensor_tensor(out=a, in0=r, scalar=-0.5, in1=r, op0=ALU.mult, op1=ALU.mult))
                    chain.link(eng.tensor_tensor(b, a, v, ALU.mult))
                    chain.link(eng.scalar_tensor_tensor(out=r, in0=b, scalar=1.5, in1=r, op0=ALU.add, op1=ALU.mult))
                for t in range(tiles):
                    last = eng.tensor_scalar(xn[:, t, :], src[:, t, :], mean[:, t:t + 1], r[:, t:t + 1],
                                             ALU.subtract, ALU.mult)
                last.then_inc(done, 1)

            NORM = 16

            def add_normalised(layer, unit, tiles, number):
                if layer:
                    eng.wait_ge(xn_done, number)
                    chain.link(eng.tensor_tensor(tiles, tiles, xn[:, 0:TILES, :], ALU.add))

            def low_x(layer, unit, slot, number):
                bank, _, made = mark_of(layer, unit, ("x_t", 0))
                eng.wait_ge(xt_hi_done, number)
                eng.tensor_tensor(xt_lo[:, slot, 0:SEQ], proj[bank][:, 0:SEQ], xt_hi[:, slot, 0:SEQ].bitcast(F32),
                                  ALU.subtract).then_inc(proj_free[bank], 1)

            def take_v(layer, unit, i, slot):
                bank, _, made = mark_of(layer, unit, ("v", i))
                eng.wait_ge(proj_made, made)
                eng.tensor_copy(values[:, slot, i // 2, (i % 2) * 512:(i % 2 + 1) * 512], proj[bank][:, :])\
                   .then_inc(proj_free[bank], 1)

            def low_y(layer, unit, h):
                n = (unit or Unit(0, 0)).count(HEADS, BATCH * HEADS * layer + h)
                bank, _, _ = mark_of(layer, unit, ("y", h))
                eng.wait_ge(y_hi_done, n + 1)
                eng.tensor_tensor(y_lo[:, h % 2, :], proj[bank][:, 0:SEQ], y_hi[:, h % 2, :].bitcast(F32),
                                  ALU.subtract).then_inc(proj_free[bank], 1)

            def maxima(layer, unit, h):
                n = unit.count(HEADS, BATCH * HEADS * layer + h)
                slot = (unit.par + h // HEADS) % 2
                hh = h % HEADS
                eng.wait_ge(score_made, n + 1)
                if layer:
                    last = eng.tensor_reduce(negmax[:, slot, hh, :], score[h % 2][:, :].rearrange("p (t k) -> p t k", t=TILES),
                                             AX.X, ALU.max, negate=True)
                else:
                    for t in range(TILES):
                        last = eng.tensor_reduce(negmax[:, slot, hh, t:t + 1], score[h % 2][:, t * SEQ:t * SEQ + (t + 1) * P],
                                                 AX.X, ALU.max, negate=True)
                last.then_inc(max_done, 1)

            def reciprocals(layer, unit, p):
                eng.wait_ge(exp_done, unit.count(HEADS, BATCH * HEADS * layer + 2 * p + 2))
                g = unit.count(PAIRS, BATCH * PAIRS * layer + p)
                eng.reciprocal(rec[:, p % 2, :, :], sums[:, unit.par, 2 * p:2 * p + 2, :].rearrange("p h t -> p t h"))\
                   .then_inc(rec_small, 1)
                eng.wait_ge(rec_small, g + 1)
                eng.tensor_copy(rec_wide[:, p % 2, :, :, :], rec[:, p % 2, :, :].unsqueeze(3).to_broadcast([P, TILES, 2, DH]))\
                   .then_inc(rec_done, 1)

            def take_probs(layer, unit, h):
                n = unit.count(HEADS, BATCH * HEADS * layer + h)
                eng.wait_ge(turn_made, n + 1)
                if layer:
                    last = eng.tensor_copy(probs_t[:, h % 4, :, :].rearrange("p t k -> p (t k)"), turn[h % 2][:, :])
                else:
                    eng.tensor_copy(probs_t[:, h % 4, 0, :], turn[h % 2][:, 0:SEQ])
                    last = eng.tensor_copy(probs_t[:, h % 4, 1, P:SEQ], turn[h % 2][:, SEQ + P:2 * SEQ])
                last.then_inc(turn_done, 1)

            def norm(layer, unit, p):
                g = unit.count(PAIRS, BATCH * PAIRS * layer + p)
                bank, frees, _ = mark_of(layer, unit, ("rsum", p))
                eng.wait_ge(proj_free[bank], frees)
                eng.wait_ge(heads_made, g + 1)
                if p == 0:
                    wait(eng, cat_lo_done, unit.count(PAIRS, BATCH * PAIRS * layer - PAIRS))
                slot = unit.par if p >= 0 else 1 - unit.par
                eng.tensor_tensor(cat[:, slot, p % PAIRS, :], heads_out[p % 2][:, 0:SEQ], rsum[:, p % 2, :], ALU.mult)\
                   .then_inc(norm_done, 1)

            def add_out(layer, unit, tiles):
                bank, _, made = mark_of(layer, unit, ("out_t", 0))
                eng.wait_ge(proj_made, made)
                eng.tensor_tensor(tiles, tiles, proj[bank][:, 0:SEQ].rearrange("p (t d) -> p t d", t=TILES), ALU.add)\
                   .then_inc(proj_free[bank], 1)

            def dve_attention(layer, links):
                start = Unit(0, 0, first=True)
                chain.at(links)
                normalise(tiles_of(None, 0, TILES), TILES, xn_done)
                add_normalised(layer, None, tiles_of(None, 0, TILES), BATCH * layer + 1)
                per = NORM + layer
                assert chain.k == per
                low_x(layer, None, 0, BATCH * layer + 1)
                take_v(layer, None, 1, 0)
                take_v(layer, None, 3, 0)
                low_y(layer, None, 0)
                low_y(layer, None, 1)
                maxima(layer, start, 0)
                low_y(layer, None, 2)
                maxima(layer, start, 1)

                def unit_work(unit):
                    for h, step in enumerate(attention_stream(unit.first, unit.last)):
                        if h % 2:
                            reciprocals(layer, unit, h // 2)
                        take_probs(layer, unit, h)
                        if ("y", h + 3) in step:
                            low_y(layer, unit, h + 3)
                        if ("scores", h + 2) in step:
                            maxima(layer, unit, h + 2)
                        if ("av", h // 2 - 1) in step:
                            norm(layer, unit, h // 2 - 1)
                        if h == 6 and not unit.last:
                            chain.at(unit.count(per, links + per))
                            normalise(tiles_of(unit, 1, TILES), TILES, xn_done)
                            add_normalised(layer, unit, tiles_of(unit, 1, TILES), unit.count(1, BATCH * layer + 2))
                        if ("x_t", 0) in step:
                            low_x(layer, unit, 1 - unit.par, unit.count(1, BATCH * layer + 2))
                        for i in (1, 3):
                            if ("v", i) in step:
                                take_v(layer, unit, i, 1 - unit.par)
                        if ("out_t", 0) in step:
                            add_out(layer, unit, tiles_of(unit, -1, TILES))
                each_unit(eng, BATCH, unit_work)
                norm(layer, END, -1)
                add_out(layer, END, x[:, (BATCH - 1) * TILES:BATCH * TILES, :])
                return links + per * BATCH

            def dve_ffn(layer, links):
                def low_fx(unit, slot, number):
                    eng.wait_ge(fxt_hi_done, number)
                    eng.tensor_tensor(xt_lo[:, slot, :], misc[:, :], xt_hi[:, slot, :].bitcast(F32), ALU.subtract)\
                       .then_inc(misc_free, 1)

                def shift_logits(unit):
                    eng.wait_ge(misc_made, misc_use(layer, unit, "logits") + 1)
                    lg = misc[:, 0:FTILES * EXPERTS].rearrange("p (t e) -> p t e", e=EXPERTS)
                    chain.link(eng.tensor_reduce(top[:, 0, :], lg, AX.X, ALU.max))
                    eng.tensor_tensor(prob_r[:, 0, :, :], lg, wide_top(0), ALU.subtract).then_inc(misc_free, 1)

                def wide_top(i):
                    return top[:, i, :].unsqueeze(2).to_broadcast([P, FTILES, EXPERTS])

                e, p, key, kept = (prob_r[:, i, :, :] for i in (1, 0, 2, 3))

                def router_softmax(number):
                    eng.wait_ge(router_exp, number)
                    chain.link(eng.tensor_reduce(top[:, 0, :], e, AX.X, ALU.add))
                    chain.link(eng.reciprocal(top[:, 1, :], top[:, 0, :]))
                    chain.link(eng.tensor_tensor(p, e, wide_top(1), ALU.mult))

                def router_pick(i):
                    left = e if i else p
                    chain.link(eng.tensor_reduce(top[:, 2, :], left, AX.X, ALU.max))
                    chain.link(eng.tensor_tensor(key, left, wide_top(2), ALU.is_equal))
                    chain.link(eng.tensor_tensor(key, key, rank[:, :, :], ALU.mult))
                    chain.link(eng.tensor_reduce(top[:, 2, :], key, AX.X, ALU.max))
                    chain.link(eng.tensor_tensor(key, rank[:, :, :], wide_top(2), ALU.is_equal))
                    if i == 0:
                        chain.link(eng.tensor_tensor(kept, key, p, ALU.mult))
                        chain.link(eng.scalar_tensor_tensor(out=e, in0=key, scalar=-2.0, in1=p, op0=ALU.mult, op1=ALU.add))

                def router_parts():
                    chain.link(eng.tensor_tensor(key, key, p, ALU.mult))
                    chain.link(eng.tensor_tensor(kept, kept, key, ALU.add))
                    parts = [cw_parts[:, :, i, :] for i in range(3)]
                    chain.link(eng.tensor_copy(parts[0], kept))
                    chain.link(eng.tensor_tensor(kept, kept, parts[0], ALU.subtract))
                    chain.link(eng.tensor_copy(parts[1], kept))
                    eng.tensor_tensor(parts[2], kept, parts[1], ALU.subtract).then_inc(cw_done, 1)

                def hidden(unit, f):
                    k = unit.count(FBLOCKS, FUNITS * FBLOCKS * layer + f)
                    b = (unit.par * FBLOCKS + f) % 2
                    slot = (unit.par * FBLOCKS + f) % 3
                    eng.wait_ge(silu_done, k + 1)
                    eng.wait_ge(up_made, k + 1)
                    wait(eng, hid_lo_done, k - 2)
                    eng.tensor_tensor(hid[:, slot, :], up[b][:, :], silu[:, b, :], ALU.mult).then_inc(gated, 1)
                    if f < FPAIRS:
                        eng.wait_ge(spread_made, unit.count(FPAIRS, FUNITS * FPAIRS * layer + f) + 1)
                        eng.wait_ge(gated, k + 1)
                        eng.tensor_tensor(hid[:, slot, :], spread[:, :], hid[:, slot, :], ALU.mult).then_inc(weighted, 1)

                def add_fout(unit, tiles):
                    eng.wait_ge(misc_made, misc_use(layer, unit, "out") + 1)
                    eng.tensor_tensor(tiles, tiles, misc[:, :].rearrange("p (t d) -> p t d", t=FTILES), ALU.add)\
                       .then_inc(misc_free, 1)

                return low_fx, shift_logits, router_softmax, router_pick, router_parts, hidden, add_fout

            def run_ffn(layer, links):
                low_fx, shift_logits, router_softmax, router_pick, router_parts, hidden, add_fout = dve_ffn(layer, links)
                start = FUNITS * layer
                PER = NORM + FROUTER
                chain.at(links)
                normalise(tiles_of(None, 0, FTILES), FTILES, fxn_done)
                low_fx(None, 0, start + 1)
                shift_logits(None)
                router_softmax(start + 1)
                router_pick(0)
                router_pick(1)
                router_parts()
                assert chain.k == PER, chain.k

                def unit_work(unit):
                    for f in range(FBLOCKS):
                        hidden(unit, f)
                        if f == 0 and not unit.last:
                            chain.at(unit.count(PER, links + PER))
                            normalise(tiles_of(unit, 1, FTILES), FTILES, fxn_done)
                        if f == 4 and not unit.first:
                            add_fout(unit, tiles_of(unit, -1, FTILES))
                        if not unit.last:
                            if f == 2:
                                low_fx(unit, 1 - unit.par, unit.count(1, start + 2))
                            if f == 3:
                                shift_logits(unit)
                            if f == 4:
                                router_softmax(unit.count(1, start + 2))
                            if f == 5:
                                router_pick(0)
                            if f == 6:
                                router_pick(1)
                            if f == 7:
                                router_parts()
                                assert chain.k == PER, chain.k
                each_unit(eng, FUNITS, unit_work)
                add_fout(FEND, x[:, (FUNITS - 1) * FTILES:FUNITS * FTILES, :])
                return links + PER * FUNITS

            FROUTER = 1 + 3 + 5 + 2 + 5 + 2 + 3
            eng.wait_ge(consts, 12 + EXPERTS)
            prep_dve(eng, 0)
            eng.wait_ge(loaded_x, 32)
            links = dve_attention(0, 0)
            before_layer(eng, 0)
            prep_dve(eng, 1)
            links = run_ffn(0, links)
            before_ffn_end(eng, 0)
            prep_dve(eng, 2)
            links = dve_attention(1, links)
            before_layer(eng, 1)
            run_ffn(1, links)


_INS = ["L0_attn_a_x", "L0_attn_a_w_q", "L0_attn_a_w_k", "L0_attn_a_w_v", "L0_attn_a_w_o", "L0_attn_b_Wq", "L0_attn_b_Wk",
        "L0_attn_b_Wv", "L0_attn_b_Wpost", "L0_ffn_Wr", "L0_ffn_Wg", "L0_ffn_Wu", "L0_ffn_Wd", "L0_ffn_Sg", "L0_ffn_Su",
        "L0_ffn_Sd"]


def kernel(**inputs):
    import numpy as _np
    import concourse.bacc as _bacc
    from concourse import mybir as _mybir
    from concourse.bass_utils import run_bass_kernel_spmd as _run

    nc = _bacc.Bacc("TRN2", target_bir_lowering=False, num_devices=1)
    arrays, args = {}, []
    for name in _INS:
        a = _np.ascontiguousarray(inputs[name])
        arrays[f"in_{name}"] = a
        args.append(nc.dram_tensor(f"in_{name}", a.shape, _mybir.dt.from_np(a.dtype), kind="ExternalInput").ap())
    y = nc.dram_tensor("out_x", (BATCH, SEQ, P), _mybir.dt.float32, kind="ExternalOutput").ap()
    build_program(nc, *args, y)
    r = _run(nc, [arrays], core_ids=[0])
    return r.results[0]["out_x"]
```

```python
from contextlib import ExitStack

import concourse.bass as bass
from concourse import mybir

F32 = mybir.dt.float32
F32R = mybir.dt.float32r
BF16 = mybir.dt.bfloat16
I32 = mybir.dt.int32
ALU = mybir.AluOpType
ACT = mybir.ActivationFunctionType
AX = mybir.AxisListType

P = 128
BATCH, SEQ = 16, 256
TILES = SEQ // P
HEADS, DH = 16, 64
PAIRS = HEADS // 2
EXPERTS = 16
EPS = 1e-5
SCALE = 1.0 / 8.0
NEG = -3.0e38

V_PARTS = 4
O_PARTS = 4
NEXT_USES = 1 + V_PARTS
SIDE_USES = NEXT_USES + 2
Y_AHEAD, S_AHEAD = 5, 3

FTOK = 512
FTILES = FTOK // P
FUNITS = BATCH * SEQ // FTOK
FPAIRS = EXPERTS // 2
FBLOCKS = FPAIRS + 1
FLAG = 3
MISC_USES = 4


class Unit:

    def __init__(self, it, c, first=False, last=False, end=False):
        self.it, self.c, self.first, self.last, self.end = it, c, first, last, end
        self.par = c % 2

    def count(self, per, plus):
        return self.it * (2 * per) + (per * self.c + plus)


def wait(eng, sem, value):
    if isinstance(value, int) and value <= 0:
        return
    eng.wait_ge(sem, value)


def each_unit(eng, units, body):
    body(Unit(0, 0, first=True))
    with eng.Fori(0, (units - 2) // 2) as it:
        body(Unit(it, 1))
        body(Unit(it, 2))
    body(Unit((units - 2) // 2, 1, last=True))


def attention_stream(first, last):
    out = []
    for h in range(HEADS):
        step = [("probs_t", h)]
        if not last and 7 <= h < 7 + V_PARTS:
            step.append(("v", h - 7))
        if not first and 11 <= h < 11 + O_PARTS:
            step.append(("out", h - 11))
        if h + S_AHEAD < HEADS or not last:
            step.append(("scores", h + S_AHEAD))
        if h + Y_AHEAD < HEADS or not last:
            step.append(("y", h + Y_AHEAD))
        if h % 2 == 0 and (h or not first):
            step.append(("av", h // 2 - 1))
        if not last and h == 5:
            step.append(("x_t", 0))
        if not first and h == 15:
            step.append(("out_t", 0))
        out.append(step)
    return out


SPLITS = {2: 0, 3: 1, 5: 2, 6: 3, 8: 4, 9: 5, 11: 6, 12: 7}

PROLOGUE = [("x_t", 0)] + [("v", i) for i in range(V_PARTS)]\
    + [("y", 0), ("y", 1), ("scores", 0), ("y", 2), ("scores", 1), ("y", 3), ("scores", 2), ("y", 4)]
SIDE = ("x_t", "v", "out", "out_t")


def build_program(nc, x_in, wq_a, wk_a, wv_a, wo_a, wq_b, wk_b, wv_b, wo_b, wr, wg, wu, wd, sg, su, sd, out):
    ctx = ExitStack()
    with ctx:
        def sb(name, shape, dt=F32):
            return ctx.enter_context(nc.sbuf_tensor(name, shape, dt))

        def sem(name):
            return ctx.enter_context(nc.semaphore(name))

        x = sb("x", [P, BATCH * TILES, P])
        ident = sb("ident", [P, P])
        zero = sb("zero", [P, 1])
        ident_b = sb("ident_b", [P, P], BF16)
        causal = sb("causal", [P, P], BF16)
        select = sb("select", [3 * EXPERTS, FPAIRS, P], BF16)
        rank = sb("rank", [P, FTILES, EXPERTS])

        m_hi = sb("m_hi", [P, HEADS, P], F32R)
        m_lo = sb("m_lo", [P, HEADS, P], F32R)
        v_hi = sb("v_hi", [P, HEADS * DH], F32R)
        v_lo = sb("v_lo", [P, HEADS * DH], F32R)
        o_hi = sb("o_hi", [P, PAIRS, P], F32R)
        o_lo = sb("o_lo", [P, PAIRS, P], F32R)
        raw_b = sb("raw_b", [P, 4, HEADS * DH])

        g_hi = sb("g_hi", [P, FBLOCKS, P], F32R)
        g_lo = sb("g_lo", [P, FBLOCKS, P], F32R)
        u_hi = sb("u_hi", [P, FBLOCKS, P], F32R)
        u_lo = sb("u_lo", [P, FBLOCKS, P], F32R)
        d_hi = sb("d_hi", [P, FBLOCKS, P], F32R)
        d_lo = sb("d_lo", [P, FBLOCKS, P], F32R)
        r_hi = sb("r_hi", [P, EXPERTS], F32R)
        r_lo = sb("r_lo", [P, EXPERTS], F32R)
        raw_f = sb("raw_f", [P, 3, FBLOCKS, P])
        raw_r = sb("raw_r", [P, EXPERTS])

        xt_hi = sb("xt_hi", [P, 2, FTOK], F32R)
        xt_lo = sb("xt_lo", [P, 2, FTOK], F32R)
        wide = sb("wide", [P, 4, HEADS * DH])
        y_hi = sb("y_hi", [P, 2, SEQ], F32R)
        y_lo = sb("y_lo", [P, 2, SEQ], F32R)
        probs = sb("probs", [P, 4, TILES, SEQ])
        probs_t = sb("probs_t", [P, 4, TILES * SEQ])
        cat = sb("cat", [P, 2, PAIRS, SEQ])
        cat_hi = sb("cat_hi", [P, PAIRS, SEQ], F32R)
        cat_lo = sb("cat_lo", [P, PAIRS, SEQ], F32R)
        sums = sb("sums", [P, 4, TILES])
        negmax = sb("negmax", [P, 4, TILES])
        rec = sb("rec", [P, 4, TILES])
        out_s = sb("out_s", [P, SEQ])
        xn = sb("xn", [P, FTILES, P])
        stats = sb("stats", [P, FTILES, 6])
        moments = sb("moments", [P, 3, FTILES])
        var = sb("var", [P, FTILES])
        newton = sb("newton", [P, 3, FTILES])
        prob_r = sb("prob_r", [P, 4, FTILES, EXPERTS])
        top = sb("top", [P, 4, FTILES])
        cw_parts = sb("cw_parts", [P, FTILES, P // EXPERTS, EXPERTS], BF16)
        cw_t = sb("cw_t", [3 * EXPERTS, 2, FTOK], BF16)

        values = wide[:, :, :].rearrange("p (s t) n -> p s t n", s=2)
        flat = wide[:, :, :].rearrange("p a n -> p (a n)")
        silu = flat[:, 0:2 * FTOK].rearrange("p (r n) -> p r n", r=2)
        hid = flat[:, 2 * FTOK:5 * FTOK].rearrange("p (r n) -> p r n", r=3)
        fout_s = flat[:, 5 * FTOK:6 * FTOK]
        hid_hi = cat_hi[:, :, :].rearrange("p a n -> p (a n)")[:, 0:3 * FTOK].rearrange("p (r n) -> p r n", r=3)
        hid_lo = cat_lo[:, :, :].rearrange("p a n -> p (a n)")[:, 0:3 * FTOK].rearrange("p (r n) -> p r n", r=3)

        banks = [ctx.enter_context(nc.psum_tensor(f"bank{i}", [P, 512], F32)) for i in range(8)]
        proj, score, turn, side = banks[0:2], banks[2:4], banks[4:6], banks[7]
        heads_out = banks[6]
        gate, up, spread, misc, acc = banks[0:2], banks[2:4], banks[4], banks[5], banks[6:8]
        misc_b = misc[:, :].bitcast(BF16)

        loaded_x = sem("loaded_x")
        loaded_a = sem("loaded_a")
        loaded_b = sem("loaded_b")
        loaded_f = sem("loaded_f")
        stored = sem("stored")
        consts = sem("consts")
        prep_made = sem("prep_made")
        prep_hi = sem("prep_hi")
        prep_lo = sem("prep_lo")
        prep_turned = sem("prep_turned")
        dve_chain = sem("dve_chain")

        side_made = sem("side_made")
        side_free = sem("side_free")
        y_made = sem("y_made")
        y_lo_done = sem("y_lo_done")
        score_made = sem("score_made")
        turn_made = sem("turn_made")
        heads_made = sem("heads_made")
        xt_hi_done = sem("xt_hi_done")
        y_hi_done = sem("y_hi_done")
        exp_done = sem("exp_done")
        gelu_done = sem("gelu_done")
        xn_done = sem("xn_done")
        max_done = sem("max_done")
        turn_done = sem("turn_done")
        rec_done = sem("rec_done")
        scaled = sem("scaled")
        heads_taken = sem("heads_taken")
        cat_hi_done = sem("cat_hi_done")
        cat_lo_done = sem("cat_lo_done")

        gate_made = sem("gate_made")
        up_made = sem("up_made")
        spread_made = sem("spread_made")
        down_made = sem("down_made")
        misc_made = sem("misc_made")
        misc_free = sem("misc_free")
        fxt_hi_done = sem("fxt_hi_done")
        silu_done = sem("silu_done")
        hid_hi_done = sem("hid_hi_done")
        router_exp = sem("router_exp")
        fout_done = sem("fout_done")
        fxn_done = sem("fxn_done")
        gated = sem("gated")
        weighted = sem("weighted")
        cw_done = sem("cw_done")
        hid_lo_done = sem("hid_lo_done")

        block = ctx.enter_context(nc.Block())

        POS = {(f, l): [e for s in attention_stream(f, l) for e in s if e[0] in SIDE and (e[0] != "out" or e[1] == 0)]
               for f, l in ((True, False), (False, False), (False, True))}

        def side_use(layer, unit, event):
            start = LAYER_USES * layer
            if unit is None:
                return start + PROLOGUE.index(event)
            if unit.end:
                return start + LAYER_USES - 2 + (event[0] == "out_t")
            pos = POS[(unit.first, unit.last)].index(event)
            if unit.first:
                return start + NEXT_USES + pos
            return unit.count(SIDE_USES, start + 2 * NEXT_USES - SIDE_USES + pos)

        LAYER_USES = BATCH * SIDE_USES

        def before_layer(eng, layer):
            eng.wait_ge(side_free, LAYER_USES * (layer + 1))

        def turned(layer, k, q):
            at = (k * TILES + q - (0 if layer else k)) * P
            return slice(at, at + P)

        END = Unit(BATCH // 2, 0, end=True)
        FEND = Unit(FUNITS // 2, 0, end=True)
        FL = FUNITS * MISC_USES

        def misc_use(layer, unit, what):
            if unit is None:
                return FL * layer + ("x", "logits", "cw").index(what)
            if unit.end:
                return FL * (layer + 1) - 1
            if unit.first:
                return FL * layer + 3 + ("x", "logits", "cw").index(what)
            order = ("out",) if unit.last else ("x", "logits", "out", "cw")
            return unit.count(MISC_USES, FL * layer + 2 + order.index(what))

        def before_ffn_end(eng, layer):
            eng.wait_ge(misc_free, FL * (layer + 1))

        raw_a = wide

        def attention_jobs(layer):
            jobs = []
            if layer == 0:
                q_rows, k_rows = raw_a[:, 0, :], raw_a[:, 1, :]
                for c in range(2):
                    jobs.append((("turn", [raw_a[:, 2, (4 * c + j) * P:(4 * c + j + 1) * P] for j in range(4)]), None, 1.0,
                                 v_hi[:, c * 512:(c + 1) * 512], v_lo[:, c * 512:(c + 1) * 512]))
                for c in range(2):
                    jobs.append((("turn", [raw_a[:, 3, (4 * c + j) * P:(4 * c + j + 1) * P] for j in range(4)]), None, 1.0,
                                 o_hi[:, 4 * c:4 * c + 4, :].rearrange("p a n -> p (a n)"),
                                 o_lo[:, 4 * c:4 * c + 4, :].rearrange("p a n -> p (a n)")))
            else:
                q_rows, k_rows = wide[:, 0, :], wide[:, 1, :]
                for c in range(2):
                    jobs.append((None, raw_b[:, 2, c * 512:(c + 1) * 512], 1.0,
                                 v_hi[:, c * 512:(c + 1) * 512], v_lo[:, c * 512:(c + 1) * 512]))
                for c in range(2):
                    jobs.append((None, raw_b[:, 3, c * 512:(c + 1) * 512], 1.0,
                                 o_hi[:, 4 * c:4 * c + 4, :].rearrange("p a n -> p (a n)"),
                                 o_lo[:, 4 * c:4 * c + 4, :].rearrange("p a n -> p (a n)")))
            for c in range(4):
                heads = [8 * (c // 2) + 2 * j + c % 2 for j in range(4)]
                pairs = [(q_rows[DH * (h % 2):DH * (h % 2) + DH, (h // 2) * P:(h // 2 + 1) * P],
                          k_rows[DH * (h % 2):DH * (h % 2) + DH, (h // 2) * P:(h // 2 + 1) * P]) for h in heads]
                jobs.append((("product", pairs), None, SCALE,
                             m_hi[:, heads[0]:heads[-1] + 1:2, :], m_lo[:, heads[0]:heads[-1] + 1:2, :]))
            return jobs

        def ffn_jobs():
            jobs = []
            for w, (hi, lo) in enumerate(((g_hi, g_lo), (u_hi, u_lo), (d_hi, d_lo))):
                for a, b in ((0, 4), (4, 8), (8, 9)):
                    jobs.append((None, raw_f[:, w, a:b, :].rearrange("p a n -> p (a n)"), 1.0,
                                 hi[:, a:b, :].rearrange("p a n -> p (a n)"), lo[:, a:b, :].rearrange("p a n -> p (a n)")))
            jobs.append((None, raw_r[:, :], 1.0, r_hi[:, :], r_lo[:, :]))
            return jobs

        JOBS = [attention_jobs(0), ffn_jobs(), attention_jobs(1)]
        JOB_START = [0, len(JOBS[0]), len(JOBS[0]) + len(JOBS[1])]
        MADE_START = [0, len(JOBS[0]), len(JOBS[0])]

        def prep_pe(eng, stage):
            made = MADE_START[stage]
            for i, (work, _, _, hi, _) in enumerate(JOBS[stage]):
                if work is None:
                    continue
                bank = banks[i % 4]
                if i >= 4 and JOBS[stage][i - 4][0] is not None:
                    eng.wait_ge(prep_lo, JOB_START[stage] + i - 3)
                for j, piece in enumerate(work[1]):
                    dst = bank[:, j * P:(j + 1) * P]
                    if work[0] == "turn":
                        last = eng.transpose(dst, piece, ident[:, :])
                    else:
                        last = eng.matmul(dst, piece[0], piece[1], start=True, stop=True)
                made += 1
                last.then_inc(prep_made, 1)

        def job_source(stage, i):
            work, src, _, hi, _ = JOBS[stage][i]
            if work is None:
                return src
            if work[0] == "product":
                return banks[i % 4][:, :].rearrange("p (a n) -> p a n", a=4)
            return banks[i % 4][:, :]

        def prep_act(eng, stage):
            made = MADE_START[stage]
            for i, (work, _, scale, hi, _) in enumerate(JOBS[stage]):
                if work is not None:
                    made += 1
                    eng.wait_ge(prep_made, made)
                eng.activation(hi, job_source(stage, i), ACT.Copy, scale=scale).then_inc(prep_hi, 1)

        def prep_dve(eng, stage):
            for i, (work, _, scale, hi, lo) in enumerate(JOBS[stage]):
                eng.wait_ge(prep_hi, JOB_START[stage] + i + 1)
                eng.scalar_tensor_tensor(out=lo, in0=job_source(stage, i), scalar=scale, in1=hi.bitcast(F32),
                                         op0=ALU.mult, op1=ALU.subtract).then_inc(prep_lo, 1)

        def prepared(eng, stage):
            eng.wait_ge(prep_lo, JOB_START[stage] + len(JOBS[stage]))

        def turn_raw_pe(eng):
            eng.wait_ge(loaded_b, 4 * 16)
            for c in range(4):
                for j in range(4):
                    last = eng.transpose(banks[4 + c][:, j * P:(j + 1) * P],
                                         raw_b[:, c // 2, ((c % 2) * 4 + j) * P:((c % 2) * 4 + j + 1) * P], ident[:, :])
                last.then_inc(prep_turned, 1)
            eng.wait_ge(prep_turned, 8)

        def turn_raw_act(eng):
            eng.wait_ge(loaded_b, 4 * 16)
            for c in range(4):
                eng.wait_ge(prep_turned, 4)
                eng.activation(wide[:, c // 2, (c % 2) * 512:(c % 2 + 1) * 512], banks[4 + c][:, :], ACT.Copy)\
                   .then_inc(prep_turned, 1)

        @block.sync
        def _(eng):
            x_tiles = x_in.rearrange("b (t p) d -> p (b t) d", p=P)
            eng.dma_start(raw_a[:, 0, :].rearrange("p (j d) -> p j d", d=P), wq_a.rearrange("(j g) q d -> (g q) j d", g=2)).then_inc(loaded_a, 16)
            eng.dma_start(raw_a[:, 1, :].rearrange("p (j d) -> p j d", d=P), wk_a.rearrange("(j g) q d -> (g q) j d", g=2)).then_inc(loaded_a, 16)
            eng.dma_start(x[:, 0:8, :], x_tiles[:, 0:8, :]).then_inc(loaded_x, 16)
            eng.dma_start(x[:, 8:32, :], x_tiles[:, 8:32, :]).then_inc(loaded_x, 16)
            eng.dma_start(raw_f[:, 0, 0:FPAIRS, :].rearrange("p a (g f) -> p (a g) f", g=2), wg.rearrange("e d f -> d e f")).then_inc(loaded_f, 16)
            eng.dma_start(raw_f[:, 1, 0:FPAIRS, :].rearrange("p a (g f) -> p (a g) f", g=2), wu.rearrange("e d f -> d e f")).then_inc(loaded_f, 16)
            eng.dma_start(raw_f[:, 2, 0:FPAIRS, :], wd.rearrange("(a g) f d -> (g f) a d", g=2)).then_inc(loaded_f, 16)
            for w, part in enumerate((sg, su, sd)):
                eng.dma_start(raw_f[:, w, FPAIRS, :], part).then_inc(loaded_f, 16)
            eng.dma_start(raw_r[:, :], wr).then_inc(loaded_f, 16)
            for w, part in enumerate((wq_b, wk_b, wv_b)):
                eng.dma_start(raw_b[:, w, :], part).then_inc(loaded_b, 16)
            eng.dma_start(raw_b[:, 3, :].rearrange("p (j n) -> p j n", n=P), wo_b.rearrange("(j p) n -> p j n", p=P)).then_inc(loaded_b, 16)

            o_tiles = out.rearrange("b (t p) d -> p (b t) d", p=P)
            for w in range(FUNITS):
                done = FL + 2 + MISC_USES * (w + 1) + (3 if w < FUNITS - 2 else 1) if w < FUNITS - 1 else 2 * FL
                eng.wait_ge(misc_free, done)
                eng.dma_start(o_tiles[:, FTILES * w:FTILES * (w + 1), :], x[:, FTILES * w:FTILES * (w + 1), :]).then_inc(stored, 16)
            eng.wait_ge(stored, 16 * FUNITS)

        @block.gpsimd
        def _(eng):
            eng.memset(ident[:, :], 0.0).then_inc(consts, 1)
            eng.memset(ident_b[:, :], 0.0).then_inc(consts, 1)
            eng.memset(zero[:, :], 0.0).then_inc(consts, 1)
            eng.memset(causal[:, :], 0.0).then_inc(consts, 1)
            eng.memset(select[:, :, :], 0.0).then_inc(consts, 1)
            eng.memset(cw_parts[:, :, :, :], 0.0).then_inc(consts, 1)
            eng.wait_ge(consts, 6)
            for m in (ident, ident_b):
                eng.affine_select(out=m[:, :], in_=m[:, :], compare_op=ALU.not_equal, fill=1.0, base=0,
                                  pattern=[[-1, P]], channel_multiplier=1).then_inc(consts, 1)
            eng.affine_select(out=causal[:, :], in_=causal[:, :], compare_op=ALU.is_ge, fill=NEG, base=0,
                              pattern=[[-1, P]], channel_multiplier=1).then_inc(consts, 1)
            for e in range(EXPERTS):
                eng.memset(rank[:, :, e:e + 1], float(EXPERTS - e)).then_inc(consts, 1)
            for part in range(3):
                view = select[:, :, :].rearrange("p a (g f) -> p a g f", g=2)
                eng.affine_select(out=view, in_=view, compare_op=ALU.not_equal, fill=1.0, base=-EXPERTS * part,
                                  pattern=[[-2, FPAIRS], [-1, 2], [0, DH]], channel_multiplier=1).then_inc(consts, 1)
                eng.wait_ge(consts, 9 + EXPERTS + part + 1)

            def scale(layer, unit, h):
                n = unit.count(HEADS, BATCH * HEADS * layer + h)
                eng.wait_ge(rec_done, n + 1)
                if layer:
                    last = eng.tensor_tensor(probs[:, h % 4, :, :], probs[:, h % 4, :, :],
                                             rec[:, h % 4, :].unsqueeze(2).to_broadcast([P, TILES, SEQ]), ALU.mult)
                else:
                    for t in range(TILES):
                        part = probs[:, h % 4, t, 0:(t + 1) * P]
                        last = eng.tensor_tensor(part, part, rec[:, h % 4, t:t + 1].to_broadcast([P, (t + 1) * P]), ALU.mult)
                last.then_inc(scaled, 1)

            def split(layer, unit, c, wait_out):
                b = unit.count(PAIRS, BATCH * PAIRS * layer + c - PAIRS)
                slot = 1 - unit.par
                if layer == 0:
                    eng.wait_ge(heads_taken, b + 1)
                else:
                    eng.wait_ge(gelu_done, unit.count(2, -2 + c // 4 + 1))
                if wait_out is not None:
                    eng.wait_ge(side_made, wait_out)
                eng.tensor_tensor(cat_hi[:, c, :], cat[:, slot, c, :], zero[:, :].to_broadcast([P, SEQ]), ALU.subtract).then_inc(cat_hi_done, 1)
                eng.wait_ge(cat_hi_done, b + 1)
                eng.tensor_tensor(cat_lo[:, c, :], cat[:, slot, c, :], cat_hi[:, c, :].bitcast(F32), ALU.subtract)\
                   .then_inc(cat_lo_done, 1)

            def pool_attention(layer):
                for h in range(S_AHEAD - 1):
                    scale(layer, Unit(0, 0), h)

                def unit_work(unit):
                    for h in range(HEADS):
                        if h + S_AHEAD - 1 < HEADS or not unit.last:
                            scale(layer, unit, h + S_AHEAD - 1)
                        if not unit.first and h in SPLITS:
                            c = SPLITS[h]
                            out_before = None
                            if c == 0 and not (isinstance(unit.it, int) and 2 * unit.it + unit.c < 2):
                                out_before = side_use(layer, unit, ("out", 0)) - SIDE_USES + 1
                            split(layer, unit, c, out_before)
                each_unit(eng, BATCH, unit_work)
                last = Unit(BATCH // 2 - 1, 1, last=True)
                for c in range(PAIRS):
                    split(layer, END, c, side_use(layer, last, ("out", 0)) + 1 if c == 0 else None)

            def pool_ffn(layer):
                def unit_work(unit):
                    for f in range(FBLOCKS):
                        k = unit.count(FBLOCKS, FUNITS * FBLOCKS * layer + f)
                        slot = (unit.par * FBLOCKS + f) % 3
                        eng.wait_ge(hid_hi_done, k + 1)
                        eng.tensor_tensor(hid_lo[:, slot, :], hid[:, slot, :], hid_hi[:, slot, :].bitcast(F32), ALU.subtract)\
                           .then_inc(hid_lo_done, 1)
                each_unit(eng, FUNITS, unit_work)

            pool_attention(0)
            pool_ffn(0)
            pool_attention(1)
            pool_ffn(1)

        @block.scalar
        def _(eng):
            eng.dma_start(raw_a[:, 2, :].rearrange("p (j d) -> p j d", d=P), wv_a.rearrange("(j g) v d -> (g v) j d", g=2)).then_inc(loaded_a, 16)
            eng.dma_start(raw_a[:, 3, :], wo_a).then_inc(loaded_a, 16)

            def take_x(layer, unit, slot):
                eng.wait_ge(side_made, side_use(layer, unit, ("x_t", 0)) + 1)
                eng.activation(xt_hi[:, slot, 0:SEQ], side[:, 0:SEQ], ACT.Copy).then_inc(xt_hi_done, 1)

            def take_v(layer, unit, i, slot):
                eng.wait_ge(side_made, side_use(layer, unit, ("v", i)) + 1)
                eng.activation(values[:, slot, i // 2, (i % 2) * 512:(i % 2 + 1) * 512], side[:, :], ACT.Copy)\
                   .then_inc(side_free, 1)

            def take_y(layer, unit, h):
                n = unit.count(HEADS, BATCH * HEADS * layer + h)
                eng.wait_ge(y_made, n + 1)
                eng.activation(y_hi[:, h % 2, :], proj[h % 2][:, 0:SEQ], ACT.Copy).then_inc(y_hi_done, 1)

            def exps(layer, unit, h):
                n = unit.count(HEADS, BATCH * HEADS * layer + h)
                eng.wait_ge(max_done, n + 1)
                for t in range(TILES):
                    keys = SEQ if layer else (t + 1) * P
                    last = eng.activation(probs[:, h % 4, t, 0:keys], score[h % 2][:, t * SEQ:t * SEQ + keys], ACT.Exp,
                                          bias=negmax[:, h % 4, t:t + 1], accum_out=sums[:, h % 4, t:t + 1])
                last.then_inc(exp_done, 1)

            def take_heads(layer, unit, p):
                eng.wait_ge(heads_made, unit.count(PAIRS, BATCH * PAIRS * layer + p) + 1)
                if p == 0:
                    wait(eng, cat_lo_done, unit.count(PAIRS, BATCH * PAIRS * layer - PAIRS))
                slot = unit.par if p >= 0 else 1 - unit.par
                eng.activation(cat[:, slot, p % PAIRS, :], heads_out[:, 0:SEQ], ACT.Copy).then_inc(heads_taken, 1)

            def gelu(unit):
                slot = 1 - unit.par
                eng.wait_ge(heads_taken, unit.count(PAIRS, BATCH * PAIRS))
                for half in range(2):
                    part = cat[:, slot, 4 * half:4 * half + 4, :]
                    eng.activation(part, part, ACT.Gelu).then_inc(gelu_done, 1)

            def take_out(layer, unit):
                eng.wait_ge(side_made, side_use(layer, unit, ("out", 0)) + 1)
                eng.activation(out_s[:, :], side[:, 0:SEQ], ACT.Copy).then_inc(side_free, 1)

            def act_attention(layer):
                start = Unit(0, 0, first=True)
                take_x(layer, None, 0)
                for i in range(0, V_PARTS, 2):
                    take_v(layer, None, i, 0)
                for e, i in PROLOGUE:
                    if e == "y":
                        take_y(layer, start, i)
                    elif e == "scores":
                        exps(layer, start, i)

                def unit_work(unit):
                    for h, step in enumerate(attention_stream(unit.first, unit.last)):
                        if ("out", O_PARTS - 1) in step:
                            take_out(layer, unit)
                        for i in range(V_PARTS):
                            if ("v", i) in step:
                                take_v(layer, unit, i, 1 - unit.par)
                        if ("y", h + Y_AHEAD) in step:
                            take_y(layer, unit, h + Y_AHEAD)
                        if ("scores", h + S_AHEAD) in step:
                            exps(layer, unit, h + S_AHEAD)
                        if ("av", h // 2 - 1) in step:
                            take_heads(layer, unit, h // 2 - 1)
                        if layer and not unit.first and h == 1:
                            gelu(unit)
                        if ("x_t", 0) in step:
                            take_x(layer, unit, 1 - unit.par)
                each_unit(eng, BATCH, unit_work)
                take_heads(layer, END, -1)
                if layer:
                    gelu(END)
                take_out(layer, END)

            def act_ffn(layer):
                def take_fx(unit, slot):
                    eng.wait_ge(misc_made, misc_use(layer, unit, "x") + 1)
                    eng.activation(xt_hi[:, slot, :], misc[:, :], ACT.Copy).then_inc(fxt_hi_done, 1)

                def router(unit):
                    eng.wait_ge(misc_free, misc_use(layer, unit, "logits") + 1)
                    eng.activation(prob_r[:, 1, :, :], prob_r[:, 0, :, :], ACT.Exp).then_inc(router_exp, 1)

                def take_cw(unit, slot):
                    use_no = misc_use(layer, unit, "cw")
                    eng.wait_ge(misc_made, use_no + 1)
                    eng.activation(cw_t[:, slot, :], misc_b[0:3 * EXPERTS, 0:FTOK], ACT.Copy).then_inc(misc_free, 1)

                def silus(unit, f):
                    k = unit.count(FBLOCKS, FUNITS * FBLOCKS * layer + f)
                    slot = (unit.par * FBLOCKS + f) % 2
                    eng.wait_ge(gate_made, k + 1)
                    wait(eng, gated, k - 1)
                    eng.activation(silu[:, slot, :], gate[slot][:, :], ACT.Silu).then_inc(silu_done, 1)

                def high(unit, f):
                    k = unit.count(FBLOCKS, FUNITS * FBLOCKS * layer + f)
                    slot = (unit.par * FBLOCKS + f) % 3
                    if f == FBLOCKS - 1:
                        eng.wait_ge(gated, k + 1)
                    else:
                        eng.wait_ge(weighted, unit.count(FPAIRS, FUNITS * FPAIRS * layer + f) + 1)
                    wait(eng, down_made, k - 2)
                    eng.activation(hid_hi[:, slot, :], hid[:, slot, :], ACT.Copy).then_inc(hid_hi_done, 1)

                def take_fout(unit):
                    slot = 1 - unit.par
                    eng.wait_ge(down_made, unit.count(FBLOCKS, FUNITS * FBLOCKS * layer))
                    eng.activation(fout_s, acc[slot][:, :], ACT.Copy).then_inc(fout_done, 1)

                take_fx(None, 0)
                router(None)
                take_cw(None, 0)

                def unit_work(unit):
                    for f in range(FBLOCKS):
                        silus(unit, f)
                        if f:
                            high(unit, f - 1)
                        if f == 3 and not unit.first:
                            take_fout(unit)
                        if not unit.last:
                            if f == 2:
                                take_fx(unit, 1 - unit.par)
                            if f == 4:
                                router(unit)
                    high(unit, FBLOCKS - 1)
                    if not unit.last:
                        take_cw(unit, 1 - unit.par)
                each_unit(eng, FUNITS, unit_work)
                take_fout(FEND)

            eng.wait_ge(loaded_a, 4 * 16)
            prep_act(eng, 0)
            act_attention(0)
            before_layer(eng, 0)
            eng.wait_ge(loaded_f, 7 * 16)
            prep_act(eng, 1)
            act_ffn(0)
            before_ffn_end(eng, 0)
            turn_raw_act(eng)
            prep_act(eng, 2)
            act_attention(1)
            before_layer(eng, 1)
            act_ffn(1)

        @block.tensor
        def _(eng):
            def claim(layer, unit, event):
                wait(eng, side_free, side_use(layer, unit, event))

            def three(dst, a_hi, a_lo, b_hi, b_lo, start=True, stop=True, masked=None):
                eng.matmul(dst, a_hi, b_hi, start=start, stop=False)
                if masked is not None:
                    eng.matmul(masked, ident_b[:, :], causal[:, :], start=False, stop=False, skip_group_check=True)
                eng.matmul(dst, a_hi, b_lo, start=False, stop=False)
                return eng.matmul(dst, a_lo, b_hi, start=False, stop=stop)

            def attention(layer):
                def x_t(unit, number):
                    claim(layer, unit, ("x_t", 0))
                    eng.wait_ge(xn_done, number)
                    for t in range(TILES):
                        last = eng.transpose(side[:, t * P:(t + 1) * P], xn[:, t, :], ident[:, :])
                    last.then_inc(side_made, 1)

                def v(unit, i, slot):
                    claim(layer, unit, ("v", i))
                    tok = slice((i // 2) * P, (i // 2 + 1) * P)
                    cols = slice((i % 2) * 512, (i % 2 + 1) * 512)
                    three(side[:, :], xt_hi[:, slot, tok], xt_lo[:, slot, tok], v_hi[:, cols], v_lo[:, cols])\
                        .then_inc(side_made, 1)

                def y(unit, h):
                    n = unit.count(HEADS, BATCH * HEADS * layer + h)
                    slot = (unit.par + h // HEADS) % 2
                    wait(eng, y_lo_done, n - 1)
                    three(proj[h % 2][:, 0:SEQ], m_hi[:, h % HEADS, :], m_lo[:, h % HEADS, :],
                          xt_hi[:, slot, 0:SEQ], xt_lo[:, slot, 0:SEQ]).then_inc(y_made, 1)

                def scores(unit, h):
                    n = unit.count(HEADS, BATCH * HEADS * layer + h)
                    slot = (unit.par + h // HEADS) % 2
                    eng.wait_ge(y_lo_done, n + 1)
                    wait(eng, exp_done, n - 1)
                    for t in range(TILES):
                        keys = SEQ if layer else (t + 1) * P
                        dst = score[h % 2][:, t * SEQ:t * SEQ + keys]
                        q = slice(t * P, (t + 1) * P)
                        diagonal = None if layer else score[h % 2][:, t * SEQ + t * P:t * SEQ + (t + 1) * P]
                        last = three(dst, y_hi[:, h % 2, q], y_lo[:, h % 2, q], xt_hi[:, slot, 0:keys], xt_lo[:, slot, 0:keys],
                                     masked=diagonal)
                    last.then_inc(score_made, 1)

                def probs_turned(unit, h):
                    n = unit.count(HEADS, BATCH * HEADS * layer + h)
                    eng.wait_ge(scaled, n + 1)
                    wait(eng, turn_done, n - 1)
                    for k in range(TILES):
                        for q in range(TILES):
                            if layer or k <= q:
                                last = eng.transpose(turn[h % 2][:, turned(layer, k, q)],
                                                     probs[:, h % 4, q, k * P:(k + 1) * P], ident[:, :])
                    last.then_inc(turn_made, 1)

                def av(unit, p):
                    wait(eng, heads_taken, unit.count(PAIRS, BATCH * PAIRS * layer + p))
                    eng.wait_ge(turn_done, unit.count(HEADS, BATCH * HEADS * layer + 2 * p + 2))
                    slot = unit.par if p >= 0 else 1 - unit.par
                    for k in range(TILES):
                        q0 = 0 if layer else k * P
                        for g in range(2):
                            h = (2 * p + g) % HEADS
                            last = eng.matmul(heads_out[DH * g:DH * g + DH, q0:SEQ],
                                              values[:, slot, k, h * DH:(h + 1) * DH],
                                              probs_t[:, h % 4, turned(layer, k, q0 // P).start:turned(layer, k, TILES - 1).stop], start=(k == 0), stop=(k == TILES - 1),
                                              skip_group_check=True)
                    last.then_inc(heads_made, 1)

                def out(unit, i, b):
                    each = PAIRS // O_PARTS
                    if i == 0:
                        claim(layer, unit, ("out", 0))
                    eng.wait_ge(cat_lo_done, b + each * (i + 1))
                    for j in range(each * i, each * (i + 1)):
                        last = three(side[:, 0:SEQ], o_hi[:, j, :], o_lo[:, j, :], cat_hi[:, j, :], cat_lo[:, j, :],
                                     start=(j == 0), stop=(j == PAIRS - 1))
                    if i == O_PARTS - 1:
                        last.then_inc(side_made, 1)

                def out_t(unit):
                    claim(layer, unit, ("out_t", 0))
                    for t in range(TILES):
                        last = eng.transpose(side[:, t * P:(t + 1) * P], out_s[:, t * P:(t + 1) * P], ident[:, :])
                    last.then_inc(side_made, 1)

                start = Unit(0, 0, first=True)
                for e, i in PROLOGUE:
                    if e == "x_t":
                        x_t(None, BATCH * layer + 1)
                    elif e == "v":
                        v(None, i, 0)
                    elif e == "y":
                        y(start, i)
                    else:
                        scores(start, i)

                def unit_work(unit):
                    for step in attention_stream(unit.first, unit.last):
                        for e, i in step:
                            if e == "probs_t":
                                probs_turned(unit, i)
                            elif e == "y":
                                y(unit, i)
                            elif e == "scores":
                                scores(unit, i)
                            elif e == "av":
                                av(unit, i)
                            elif e == "out":
                                out(unit, i, unit.count(PAIRS, BATCH * PAIRS * layer - PAIRS))
                            elif e == "out_t":
                                out_t(unit)
                            elif e == "x_t":
                                x_t(unit, unit.count(1, BATCH * layer + 2))
                            else:
                                v(unit, i, 1 - unit.par)
                each_unit(eng, BATCH, unit_work)
                av(END, -1)
                for i in range(O_PARTS):
                    out(END, i, BATCH * PAIRS * (layer + 1) - PAIRS)
                out_t(END)

            def ffn(layer):
                def x_t(unit, number):
                    no = misc_use(layer, unit, "x")
                    wait(eng, misc_free, no)
                    eng.wait_ge(fxn_done, number)
                    for t in range(FTILES):
                        last = eng.transpose(misc[:, t * P:(t + 1) * P], xn[:, t, :], ident[:, :])
                    last.then_inc(misc_made, 1)

                def logits(unit, slot):
                    no = misc_use(layer, unit, "logits")
                    eng.wait_ge(misc_free, no)
                    for t in range(FTILES):
                        tok = slice(t * P, (t + 1) * P)
                        last = three(misc[:, t * EXPERTS:(t + 1) * EXPERTS], xt_hi[:, slot, tok], xt_lo[:, slot, tok],
                                     r_hi[:, :], r_lo[:, :])
                    last.then_inc(misc_made, 1)

                def cw_turned(unit, number):
                    no = misc_use(layer, unit, "cw")
                    eng.wait_ge(misc_free, no)
                    eng.wait_ge(cw_done, number)
                    for t in range(FTILES):
                        last = eng.transpose(misc_b[:, t * P:(t + 1) * P],
                                             cw_parts[:, t, :, :].rearrange("p a e -> p (a e)"), ident_b[:, :])
                    last.then_inc(misc_made, 1)

                def blocks(unit, f):
                    k = unit.count(FBLOCKS, FUNITS * FBLOCKS * layer + f)
                    b = (unit.par * FBLOCKS + f) % 2
                    xs = xt_hi[:, unit.par, :], xt_lo[:, unit.par, :]
                    wait(eng, silu_done, k - 1)
                    three(gate[b][:, :], g_hi[:, f, :], g_lo[:, f, :], *xs).then_inc(gate_made, 1)
                    wait(eng, gated, k - 1)
                    three(up[b][:, :], u_hi[:, f, :], u_lo[:, f, :], *xs).then_inc(up_made, 1)
                    if f < FPAIRS:
                        wait(eng, weighted, unit.count(FPAIRS, FUNITS * FPAIRS * layer + f))
                        eng.matmul(spread[:, :], select[:, f, :], cw_t[:, unit.par, :], start=True, stop=True)\
                           .then_inc(spread_made, 1)

                def down(unit, f):
                    k = unit.count(FBLOCKS, FUNITS * FBLOCKS * layer + f)
                    slot = (unit.par * FBLOCKS + f) % 3
                    a = unit.par if f >= 0 else 1 - unit.par
                    f %= FBLOCKS
                    eng.wait_ge(hid_lo_done, k + 1)
                    three(acc[a][:, :], d_hi[:, f, :], d_lo[:, f, :], hid_hi[:, slot, :], hid_lo[:, slot, :],
                          start=(f == 0), stop=(f == FBLOCKS - 1)).then_inc(down_made, 1)

                def out_t(unit, number):
                    no = misc_use(layer, unit, "out")
                    eng.wait_ge(misc_free, no)
                    eng.wait_ge(fout_done, number)
                    for t in range(FTILES):
                        last = eng.transpose(misc[:, t * P:(t + 1) * P], fout_s[:, t * P:(t + 1) * P], ident[:, :])
                    last.then_inc(misc_made, 1)

                x_t(None, FUNITS * layer + 1)
                logits(None, 0)
                cw_turned(None, FUNITS * layer + 1)

                def unit_work(unit):
                    for f in range(FBLOCKS):
                        if f == 0:
                            eng.wait_ge(misc_free, FL * layer + 3 if unit.first else unit.count(MISC_USES, FL * layer + 2))
                        blocks(unit, f)
                        if f >= FLAG or not unit.first:
                            down(unit, f - FLAG)
                        if not unit.last:
                            if f == 2:
                                x_t(unit, unit.count(1, FUNITS * layer + 2))
                            if f == 3:
                                logits(unit, 1 - unit.par)
                        if f == 4 and not unit.first:
                            out_t(unit, unit.count(1, FUNITS * layer))
                        if not unit.last:
                            if f == 8:
                                cw_turned(unit, unit.count(1, FUNITS * layer + 2))
                each_unit(eng, FUNITS, unit_work)
                for f in range(FLAG):
                    down(FEND, f - FLAG)
                out_t(FEND, FUNITS * (layer + 1))

            eng.wait_ge(consts, 12 + EXPERTS)
            eng.wait_ge(loaded_a, 4 * 16)
            prep_pe(eng, 0)
            prepared(eng, 0)
            attention(0)
            before_layer(eng, 0)
            prepared(eng, 1)
            ffn(0)
            before_ffn_end(eng, 0)
            turn_raw_pe(eng)
            prep_pe(eng, 2)
            prepared(eng, 2)
            attention(1)
            before_layer(eng, 1)
            ffn(1)

        @block.vector
        def _(eng):
            class Chain:

                def __init__(self):
                    self.base, self.k = 0, 0

                def at(self, value):
                    self.base, self.k = value, 0

                def link(self, ins):
                    ins.then_inc(dve_chain, 1)
                    self.k += 1
                    eng.wait_ge(dve_chain, self.base + self.k)

            chain = Chain()
            def tiles_of(unit, ahead, tiles):
                if unit is None:
                    return x[:, 0:tiles, :]
                at = unit.count(tiles, ahead * tiles)
                return x[:, at:at + tiles, :] if isinstance(at, int) else x[:, bass.ds(at, tiles), :]

            NORM_PARTS = 5
            NORM = 16

            def normalise(src, tiles, part, done):
                mean, diff, both = (moments[:, i, 0:tiles] for i in range(3))
                v, r, a, b = var[:, 0:tiles], newton[:, 0, 0:tiles], newton[:, 1, 0:tiles], newton[:, 2, 0:tiles]
                if part == 0:
                    for t in range(tiles):
                        last = eng.bn_stats(stats[:, t, :], src[:, t, :])
                    chain.link(last)
                    even, odd = stats[:, 0:tiles, 1], stats[:, 0:tiles, 4]
                    eng.tensor_tensor(mean, even, odd, ALU.add)
                    eng.tensor_tensor(diff, even, odd, ALU.subtract)
                    chain.link(eng.tensor_tensor(both, stats[:, 0:tiles, 2], stats[:, 0:tiles, 5], ALU.add))
                    eng.tensor_scalar(mean, mean, 0.5, None, ALU.mult)
                    chain.link(eng.scalar_tensor_tensor(out=diff, in0=diff, scalar=0.25, in1=diff, op0=ALU.mult, op1=ALU.mult))
                    chain.link(eng.scalar_tensor_tensor(out=both, in0=both, scalar=1.0 / P, in1=diff, op0=ALU.mult, op1=ALU.add))
                if part == 1:
                    chain.link(eng.tensor_scalar(v, both, EPS, None, ALU.add))
                    chain.link(eng.tensor_scalar(a.bitcast(I32), v.bitcast(I32), 1, None, ALU.logical_shift_right))
                    chain.link(eng.tensor_scalar(r.bitcast(I32), a.bitcast(I32), -1.0, float(0x5F3759DF), ALU.mult, ALU.add))
                if part in (1, 2, 3):
                    chain.link(eng.scalar_tensor_tensor(out=a, in0=r, scalar=-0.5, in1=r, op0=ALU.mult, op1=ALU.mult))
                    chain.link(eng.tensor_tensor(b, a, v, ALU.mult))
                    chain.link(eng.scalar_tensor_tensor(out=r, in0=b, scalar=1.5, in1=r, op0=ALU.add, op1=ALU.mult))
                if part == 4:
                    for t in range(tiles):
                        last = eng.tensor_scalar(xn[:, t, :], src[:, t, :], mean[:, t:t + 1], r[:, t:t + 1],
                                                 ALU.subtract, ALU.mult)
                    last.then_inc(done, 1)

            def add_normalised(layer, unit, tiles, number):
                if layer:
                    eng.wait_ge(xn_done, number)
                    chain.link(eng.tensor_tensor(tiles, tiles, xn[:, 0:TILES, :], ALU.add))

            def low_x(layer, unit, slot, number):
                eng.wait_ge(xt_hi_done, number)
                eng.tensor_tensor(xt_lo[:, slot, 0:SEQ], side[:, 0:SEQ], xt_hi[:, slot, 0:SEQ].bitcast(F32),
                                  ALU.subtract).then_inc(side_free, 1)

            def take_v(layer, unit, i, slot):
                eng.wait_ge(side_made, side_use(layer, unit, ("v", i)) + 1)
                eng.tensor_copy(values[:, slot, i // 2, (i % 2) * 512:(i % 2 + 1) * 512], side[:, :])\
                   .then_inc(side_free, 1)

            def low_y(layer, unit, h):
                n = unit.count(HEADS, BATCH * HEADS * layer + h)
                eng.wait_ge(y_hi_done, n + 1)
                eng.tensor_tensor(y_lo[:, h % 2, :], proj[h % 2][:, 0:SEQ], y_hi[:, h % 2, :].bitcast(F32),
                                  ALU.subtract).then_inc(y_lo_done, 1)

            def maxima(layer, unit, h):
                n = unit.count(HEADS, BATCH * HEADS * layer + h)
                eng.wait_ge(score_made, n + 1)
                if layer:
                    last = eng.tensor_reduce(negmax[:, h % 4, :], score[h % 2][:, :].rearrange("p (t k) -> p t k", t=TILES),
                                             AX.X, ALU.max, negate=True)
                else:
                    for t in range(TILES):
                        last = eng.tensor_reduce(negmax[:, h % 4, t:t + 1], score[h % 2][:, t * SEQ:t * SEQ + (t + 1) * P],
                                                 AX.X, ALU.max, negate=True)
                last.then_inc(max_done, 1)

            def reciprocals(layer, unit, h):
                eng.wait_ge(exp_done, unit.count(HEADS, BATCH * HEADS * layer + h) + 1)
                eng.reciprocal(rec[:, h % 4, :], sums[:, h % 4, :]).then_inc(rec_done, 1)

            def take_probs(layer, unit, h):
                n = unit.count(HEADS, BATCH * HEADS * layer + h)
                eng.wait_ge(turn_made, n + 1)
                cols = turned(layer, TILES - 1, TILES - 1).stop
                eng.tensor_copy(probs_t[:, h % 4, 0:cols], turn[h % 2][:, 0:cols]).then_inc(turn_done, 1)

            def add_out(layer, unit, tiles):
                eng.wait_ge(side_made, side_use(layer, unit, ("out_t", 0)) + 1)
                eng.tensor_tensor(tiles, tiles, side[:, 0:SEQ].rearrange("p (t d) -> p t d", t=TILES), ALU.add)\
                   .then_inc(side_free, 1)

            def dve_attention(layer, links):
                start = Unit(0, 0, first=True)
                chain.at(links)
                for part in range(NORM_PARTS):
                    normalise(tiles_of(None, 0, TILES), TILES, part, xn_done)
                add_normalised(layer, None, tiles_of(None, 0, TILES), BATCH * layer + 1)
                per = NORM + layer
                assert chain.k == per
                low_x(layer, None, 0, BATCH * layer + 1)
                for i in range(1, V_PARTS, 2):
                    take_v(layer, None, i, 0)
                for e, i in PROLOGUE:
                    if e == "y":
                        low_y(layer, start, i)
                    elif e == "scores":
                        maxima(layer, start, i)
                        if i:
                            reciprocals(layer, start, i - 1)

                def unit_work(unit):
                    for h, step in enumerate(attention_stream(unit.first, unit.last)):
                        take_probs(layer, unit, h)
                        if ("scores", h + S_AHEAD) in step:
                            maxima(layer, unit, h + S_AHEAD)
                        if h + S_AHEAD - 1 < HEADS or not unit.last:
                            reciprocals(layer, unit, h + S_AHEAD - 1)
                        if ("y", h + Y_AHEAD) in step:
                            low_y(layer, unit, h + Y_AHEAD)
                        if h == 0:
                            chain.at(unit.count(per, links + per))
                        if 1 <= h <= NORM_PARTS and not unit.last:
                            normalise(tiles_of(unit, 1, TILES), TILES, h - 1, xn_done)
                        if h == NORM_PARTS and not unit.last:
                            add_normalised(layer, unit, tiles_of(unit, 1, TILES), unit.count(1, BATCH * layer + 2))
                        if ("x_t", 0) in step:
                            low_x(layer, unit, 1 - unit.par, unit.count(1, BATCH * layer + 2))
                        if ("out_t", 0) in step:
                            add_out(layer, unit, tiles_of(unit, -1, TILES))
                each_unit(eng, BATCH, unit_work)
                add_out(layer, END, x[:, (BATCH - 1) * TILES:BATCH * TILES, :])
                return links + per * BATCH

            def dve_ffn(layer, links):
                def low_fx(unit, slot, number):
                    eng.wait_ge(fxt_hi_done, number)
                    eng.tensor_tensor(xt_lo[:, slot, :], misc[:, :], xt_hi[:, slot, :].bitcast(F32), ALU.subtract)\
                       .then_inc(misc_free, 1)

                def shift_logits(unit):
                    eng.wait_ge(misc_made, misc_use(layer, unit, "logits") + 1)
                    lg = misc[:, 0:FTILES * EXPERTS].rearrange("p (t e) -> p t e", e=EXPERTS)
                    chain.link(eng.tensor_reduce(top[:, 0, :], lg, AX.X, ALU.max))
                    eng.tensor_tensor(prob_r[:, 0, :, :], lg, wide_top(0), ALU.subtract).then_inc(misc_free, 1)

                def wide_top(i):
                    return top[:, i, :].unsqueeze(2).to_broadcast([P, FTILES, EXPERTS])

                e, p, key, kept = (prob_r[:, i, :, :] for i in (1, 0, 2, 3))

                def router_softmax(number):
                    eng.wait_ge(router_exp, number)
                    chain.link(eng.tensor_reduce(top[:, 0, :], e, AX.X, ALU.add))
                    chain.link(eng.reciprocal(top[:, 1, :], top[:, 0, :]))
                    chain.link(eng.tensor_tensor(p, e, wide_top(1), ALU.mult))

                def router_pick(i):
                    left = e if i else p
                    chain.link(eng.tensor_reduce(top[:, 2, :], left, AX.X, ALU.max))
                    chain.link(eng.tensor_tensor(key, left, wide_top(2), ALU.is_equal))
                    chain.link(eng.tensor_tensor(key, key, rank[:, :, :], ALU.mult))
                    chain.link(eng.tensor_reduce(top[:, 2, :], key, AX.X, ALU.max))
                    chain.link(eng.tensor_tensor(key, rank[:, :, :], wide_top(2), ALU.is_equal))
                    if i == 0:
                        chain.link(eng.tensor_tensor(kept, key, p, ALU.mult))
                        chain.link(eng.scalar_tensor_tensor(out=e, in0=key, scalar=-2.0, in1=p, op0=ALU.mult, op1=ALU.add))

                def router_parts():
                    chain.link(eng.tensor_tensor(key, key, p, ALU.mult))
                    chain.link(eng.tensor_tensor(kept, kept, key, ALU.add))
                    parts = [cw_parts[:, :, i, :] for i in range(3)]
                    chain.link(eng.tensor_copy(parts[0], kept))
                    chain.link(eng.tensor_tensor(kept, kept, parts[0], ALU.subtract))
                    chain.link(eng.tensor_copy(parts[1], kept))
                    eng.tensor_tensor(parts[2], kept, parts[1], ALU.subtract).then_inc(cw_done, 1)

                def hidden(unit, f):
                    k = unit.count(FBLOCKS, FUNITS * FBLOCKS * layer + f)
                    b = (unit.par * FBLOCKS + f) % 2
                    slot = (unit.par * FBLOCKS + f) % 3
                    eng.wait_ge(silu_done, k + 1)
                    eng.wait_ge(up_made, k + 1)
                    wait(eng, hid_lo_done, k - 2)
                    eng.tensor_tensor(hid[:, slot, :], up[b][:, :], silu[:, b, :], ALU.mult).then_inc(gated, 1)
                    if f < FPAIRS:
                        eng.wait_ge(spread_made, unit.count(FPAIRS, FUNITS * FPAIRS * layer + f) + 1)
                        eng.wait_ge(gated, k + 1)
                        eng.tensor_tensor(hid[:, slot, :], spread[:, :], hid[:, slot, :], ALU.mult).then_inc(weighted, 1)

                def add_fout(unit, tiles):
                    eng.wait_ge(misc_made, misc_use(layer, unit, "out") + 1)
                    eng.tensor_tensor(tiles, tiles, misc[:, :].rearrange("p (t d) -> p t d", t=FTILES), ALU.add)\
                       .then_inc(misc_free, 1)

                return low_fx, shift_logits, router_softmax, router_pick, router_parts, hidden, add_fout

            def run_ffn(layer, links):
                low_fx, shift_logits, router_softmax, router_pick, router_parts, hidden, add_fout = dve_ffn(layer, links)
                start = FUNITS * layer
                PER = NORM + FROUTER
                chain.at(links)
                for part in range(NORM_PARTS):
                    normalise(tiles_of(None, 0, FTILES), FTILES, part, fxn_done)
                low_fx(None, 0, start + 1)
                shift_logits(None)
                router_softmax(start + 1)
                router_pick(0)
                router_pick(1)
                router_parts()
                assert chain.k == PER, chain.k

                def unit_work(unit):
                    for f in range(FBLOCKS):
                        hidden(unit, f)
                        if f == 0 and not unit.last:
                            chain.at(unit.count(PER, links + PER))
                            for part in range(NORM_PARTS):
                                normalise(tiles_of(unit, 1, FTILES), FTILES, part, fxn_done)
                        if f == 4 and not unit.first:
                            add_fout(unit, tiles_of(unit, -1, FTILES))
                        if not unit.last:
                            if f == 2:
                                low_fx(unit, 1 - unit.par, unit.count(1, start + 2))
                            if f == 3:
                                shift_logits(unit)
                            if f == 4:
                                router_softmax(unit.count(1, start + 2))
                            if f == 5:
                                router_pick(0)
                            if f == 6:
                                router_pick(1)
                            if f == 7:
                                router_parts()
                                assert chain.k == PER, chain.k
                each_unit(eng, FUNITS, unit_work)
                add_fout(FEND, x[:, (FUNITS - 1) * FTILES:FUNITS * FTILES, :])
                return links + PER * FUNITS

            FROUTER = 1 + 3 + 5 + 2 + 5 + 2 + 3
            eng.wait_ge(consts, 12 + EXPERTS)
            prep_dve(eng, 0)
            eng.wait_ge(loaded_x, 32)
            links = dve_attention(0, 0)
            before_layer(eng, 0)
            prep_dve(eng, 1)
            links = run_ffn(0, links)
            before_ffn_end(eng, 0)
            prep_dve(eng, 2)
            links = dve_attention(1, links)
            before_layer(eng, 1)
            run_ffn(1, links)


_INS = ["L0_attn_a_x", "L0_attn_a_w_q", "L0_attn_a_w_k", "L0_attn_a_w_v", "L0_attn_a_w_o", "L0_attn_b_Wq", "L0_attn_b_Wk",
        "L0_attn_b_Wv", "L0_attn_b_Wpost", "L0_ffn_Wr", "L0_ffn_Wg", "L0_ffn_Wu", "L0_ffn_Wd", "L0_ffn_Sg", "L0_ffn_Su",
        "L0_ffn_Sd"]


def kernel(**inputs):
    import numpy as _np
    import concourse.bacc as _bacc
    from concourse import mybir as _mybir
    from concourse.bass_utils import run_bass_kernel_spmd as _run

    nc = _bacc.Bacc("TRN2", target_bir_lowering=False, num_devices=1)
    arrays, args = {}, []
    for name in _INS:
        a = _np.ascontiguousarray(inputs[name])
        arrays[f"in_{name}"] = a
        args.append(nc.dram_tensor(f"in_{name}", a.shape, _mybir.dt.from_np(a.dtype), kind="ExternalInput").ap())
    y = nc.dram_tensor("out_x", (BATCH, SEQ, P), _mybir.dt.float32, kind="ExternalOutput").ap()
    build_program(nc, *args, y)
    r = _run(nc, [arrays], core_ids=[0])
    return r.results[0]["out_x"]
```

```python
from contextlib import ExitStack

import concourse.bass as bass
from concourse import mybir

F32 = mybir.dt.float32
F32R = mybir.dt.float32r
BF16 = mybir.dt.bfloat16
I32 = mybir.dt.int32
ALU = mybir.AluOpType
ACT = mybir.ActivationFunctionType
AX = mybir.AxisListType

P = 128
BATCH, SEQ = 16, 256
TILES = SEQ // P
HEADS, DH = 16, 64
PAIRS = HEADS // 2
EXPERTS = 16
EPS = 1e-5
SCALE = 1.0 / 8.0
NEG = -3.0e38

V_PARTS = 4
O_PARTS = 4
NEXT_USES = 1 + V_PARTS
SIDE_USES = NEXT_USES + 2
Y_AHEAD, S_AHEAD = 6, 4

FTOK = 512
FTILES = FTOK // P
FUNITS = BATCH * SEQ // FTOK
FPAIRS = EXPERTS // 2
FBLOCKS = FPAIRS + 1
DOWN_LAG = 4
HIGH_LAG = 2
TOP8 = 8
NONE = -1.0
MISC_USES = 4


class Unit:

    def __init__(self, it, c, first=False, last=False, end=False):
        self.it, self.c, self.first, self.last, self.end = it, c, first, last, end
        self.par = c % 2

    def count(self, per, plus):
        return self.it * (2 * per) + (per * self.c + plus)


def wait(eng, sem, value):
    if isinstance(value, int) and value <= 0:
        return
    eng.wait_ge(sem, value)


def each_unit(eng, units, body):
    body(Unit(0, 0, first=True))
    with eng.Fori(0, (units - 2) // 2) as it:
        body(Unit(it, 1))
        body(Unit(it, 2))
    body(Unit((units - 2) // 2, 1, last=True))


def attention_stream(first, last):
    out = []
    for h in range(HEADS):
        step = [("probs_t", h)]
        if not last and 7 <= h < 7 + V_PARTS:
            step.append(("v", h - 7))
        if not first and 11 <= h < 11 + O_PARTS:
            step.append(("out", h - 11))
        if h + S_AHEAD < HEADS or not last:
            step.append(("scores", h + S_AHEAD))
        if h + Y_AHEAD < HEADS or not last:
            step.append(("y", h + Y_AHEAD))
        if h % 2 == 0 and (h or not first):
            step.append(("av", h // 2 - 1))
        if not last and h == 5:
            step.append(("x_t", 0))
        if not first and h == 15:
            step.append(("out_t", 0))
        out.append(step)
    return out


SPLITS = {2: 0, 3: 1, 5: 2, 6: 3, 8: 4, 9: 5, 11: 6, 12: 7}

PROLOGUE = [("x_t", 0)] + [("v", i) for i in range(V_PARTS)]\
    + [("y", 0), ("y", 1), ("scores", 0), ("y", 2), ("scores", 1), ("y", 3), ("scores", 2), ("y", 4),
       ("scores", 3), ("y", 5)]
SIDE = ("x_t", "v", "out", "out_t")


def build_program(nc, x_in, wq_a, wk_a, wv_a, wo_a, wq_b, wk_b, wv_b, wo_b, wr, wg, wu, wd, sg, su, sd, out):
    ctx = ExitStack()
    with ctx:
        def sb(name, shape, dt=F32):
            return ctx.enter_context(nc.sbuf_tensor(name, shape, dt))

        def sem(name):
            return ctx.enter_context(nc.semaphore(name))

        x = sb("x", [P, BATCH * TILES, P])
        ident = sb("ident", [P, P])
        zero = sb("zero", [P, 1])
        ident_b = sb("ident_b", [P, P], BF16)
        causal = sb("causal", [P, P], BF16)
        select = sb("select", [3 * EXPERTS, FPAIRS, P], BF16)


        m_hi = sb("m_hi", [P, HEADS, P], F32R)
        m_lo = sb("m_lo", [P, HEADS, P], F32R)
        v_hi = sb("v_hi", [P, HEADS * DH], F32R)
        v_lo = sb("v_lo", [P, HEADS * DH], F32R)
        o_hi = sb("o_hi", [P, PAIRS, P], F32R)
        o_lo = sb("o_lo", [P, PAIRS, P], F32R)
        raw_b = sb("raw_b", [P, 4, HEADS * DH])

        g_hi = sb("g_hi", [P, FBLOCKS, P], F32R)
        g_lo = sb("g_lo", [P, FBLOCKS, P], F32R)
        u_hi = sb("u_hi", [P, FBLOCKS, P], F32R)
        u_lo = sb("u_lo", [P, FBLOCKS, P], F32R)
        d_hi = sb("d_hi", [P, FBLOCKS, P], F32R)
        d_lo = sb("d_lo", [P, FBLOCKS, P], F32R)
        r_hi = sb("r_hi", [P, EXPERTS], F32R)
        r_lo = sb("r_lo", [P, EXPERTS], F32R)
        raw_f = sb("raw_f", [P, 3, FBLOCKS, P])
        raw_r = sb("raw_r", [P, EXPERTS])

        xt_hi = sb("xt_hi", [P, 2, FTOK], F32R)
        xt_lo = sb("xt_lo", [P, 2, FTOK], F32R)
        wide = sb("wide", [P, 4, HEADS * DH])
        y_hi = sb("y_hi", [P, 2, SEQ], F32R)
        y_lo = sb("y_lo", [P, 2, SEQ], F32R)
        probs = sb("probs", [P, 4, TILES, SEQ])
        probs_t = sb("probs_t", [P, 4, TILES * SEQ])
        cat = sb("cat", [P, 2, PAIRS, SEQ])
        cat_hi = sb("cat_hi", [P, PAIRS, SEQ], F32R)
        cat_lo = sb("cat_lo", [P, PAIRS, SEQ], F32R)
        sums = sb("sums", [P, 4, TILES])
        negmax = sb("negmax", [P, 4, TILES])
        rec = sb("rec", [P, 4, TILES])
        out_s = sb("out_s", [P, SEQ])
        xn = sb("xn", [P, FTILES, P])
        stats = sb("stats", [P, FTILES, 6])
        moments = sb("moments", [P, 3, FTILES])
        var = sb("var", [P, FTILES])
        newton = sb("newton", [P, 3, FTILES])
        prob_r = sb("prob_r", [P, 4, FTILES, EXPERTS])
        prob_w = sb("prob_w", [P, FTILES, EXPERTS + TOP8])
        rest_w = sb("rest_w", [P, FTILES, EXPERTS + TOP8])
        carrier = sb("carrier", [P, 1])
        top = sb("top", [P, 4, FTILES])
        top8 = sb("top8", [P, FTILES, TOP8])
        cw_parts = sb("cw_parts", [P, FTILES, P // EXPERTS, EXPERTS], BF16)
        cw_t = sb("cw_t", [3 * EXPERTS, 2, FTOK], BF16)

        values = wide[:, :, :].rearrange("p (s t) n -> p s t n", s=2)
        flat = wide[:, :, :].rearrange("p a n -> p (a n)")
        silu = flat[:, 0:2 * FTOK].rearrange("p (r n) -> p r n", r=2)
        hid = flat[:, 2 * FTOK:5 * FTOK].rearrange("p (r n) -> p r n", r=3)
        fout_s = flat[:, 5 * FTOK:6 * FTOK]
        hid_hi = cat_hi[:, :, :].rearrange("p a n -> p (a n)")[:, 0:3 * FTOK].rearrange("p (r n) -> p r n", r=3)
        hid_lo = cat_lo[:, :, :].rearrange("p a n -> p (a n)")[:, 0:3 * FTOK].rearrange("p (r n) -> p r n", r=3)

        banks = [ctx.enter_context(nc.psum_tensor(f"bank{i}", [P, 512], F32)) for i in range(8)]
        proj, score, turn, side = banks[0], banks[1:5], banks[5], banks[7]
        heads_out = banks[6]
        gate, up, spread, misc, acc = banks[0:2], banks[2:4], (banks[4], banks[7]), banks[5], banks[6]
        misc_b = misc[:, :].bitcast(BF16)

        loaded_first = sem("loaded_first")
        loaded_x = sem("loaded_x")
        loaded_a = sem("loaded_a")
        loaded_b = sem("loaded_b")
        loaded_f = sem("loaded_f")
        stored = sem("stored")
        consts = sem("consts")
        prep_made = sem("prep_made")
        prep_hi = sem("prep_hi")
        prep_lo = sem("prep_lo")
        prep_turned = sem("prep_turned")
        dve_chain = sem("dve_chain")

        side_made = sem("side_made")
        side_free = sem("side_free")
        y_made = sem("y_made")
        y_lo_done = sem("y_lo_done")
        score_made = sem("score_made")
        turn_made = sem("turn_made")
        heads_made = sem("heads_made")
        xt_hi_done = sem("xt_hi_done")
        y_hi_done = sem("y_hi_done")
        exp_done = sem("exp_done")
        gelu_done = sem("gelu_done")
        xn_done = sem("xn_done")
        max_done = sem("max_done")
        turn_done = sem("turn_done")
        rec_done = sem("rec_done")
        scaled = sem("scaled")
        heads_taken = sem("heads_taken")
        cat_hi_done = sem("cat_hi_done")
        cat_lo_done = sem("cat_lo_done")

        gate_made = sem("gate_made")
        up_made = sem("up_made")
        spread_made = sem("spread_made")
        down_made = sem("down_made")
        misc_made = sem("misc_made")
        misc_free = sem("misc_free")
        fxt_hi_done = sem("fxt_hi_done")
        silu_done = sem("silu_done")
        hid_hi_done = sem("hid_hi_done")
        router_exp = sem("router_exp")
        fout_done = sem("fout_done")
        fxn_done = sem("fxn_done")
        gated = sem("gated")
        weighted = sem("weighted")
        cw_done = sem("cw_done")
        hid_lo_done = sem("hid_lo_done")

        block = ctx.enter_context(nc.Block())

        POS = {(f, l): [e for s in attention_stream(f, l) for e in s if e[0] in SIDE and (e[0] != "out" or e[1] == 0)]
               for f, l in ((True, False), (False, False), (False, True))}

        def side_use(layer, unit, event):
            start = LAYER_USES * layer
            if unit is None:
                return start + PROLOGUE.index(event)
            if unit.end:
                return start + LAYER_USES - 2 + (event[0] == "out_t")
            pos = POS[(unit.first, unit.last)].index(event)
            if unit.first:
                return start + NEXT_USES + pos
            return unit.count(SIDE_USES, start + 2 * NEXT_USES - SIDE_USES + pos)

        LAYER_USES = BATCH * SIDE_USES

        def before_layer(eng, layer):
            eng.wait_ge(side_free, LAYER_USES * (layer + 1))

        def turned(layer, k, q):
            at = (k * TILES + q - (0 if layer else k)) * P
            return slice(at, at + P)

        END = Unit(BATCH // 2, 0, end=True)
        FEND = Unit(FUNITS // 2, 0, end=True)
        FL = FUNITS * MISC_USES

        def misc_use(layer, unit, what):
            if unit is None:
                return FL * layer + ("x", "logits").index(what)
            if unit.end:
                return FL * (layer + 1) - 1
            order = ("cw", "out") if unit.last else ("cw", "x", "logits", "out")
            if unit.first:
                return FL * layer + 2 + order.index(what)
            return unit.count(MISC_USES, FL * layer + 1 + order.index(what))

        def weights_before(layer, unit, f):
            return unit.count(FPAIRS, FUNITS * FPAIRS * layer + (f if f >= 0 else f + 1))

        def before_ffn_end(eng, layer):
            eng.wait_ge(misc_free, FL * (layer + 1))

        raw_a = wide
        raw_turned = cat[:, 0, :, :].rearrange("p a n -> p (a n)")

        def attention_jobs(layer):
            jobs = []
            if layer == 0:
                q_rows, k_rows = raw_a[:, 0, :], raw_a[:, 1, :]
                for c in range(2):
                    jobs.append((("turn", [raw_a[:, 2, (4 * c + j) * P:(4 * c + j + 1) * P] for j in range(4)]), None, 1.0,
                                 v_hi[:, c * 512:(c + 1) * 512], v_lo[:, c * 512:(c + 1) * 512]))
                for c in range(2):
                    jobs.append((("turn", [raw_a[:, 3, (4 * c + j) * P:(4 * c + j + 1) * P] for j in range(4)]), None, 1.0,
                                 o_hi[:, 4 * c:4 * c + 4, :].rearrange("p a n -> p (a n)"),
                                 o_lo[:, 4 * c:4 * c + 4, :].rearrange("p a n -> p (a n)")))
            else:
                q_rows, k_rows = raw_turned[:, 0:HEADS * DH], raw_turned[:, HEADS * DH:2 * HEADS * DH]
            for c in range(4):
                heads = [8 * (c // 2) + 2 * j + c % 2 for j in range(4)]
                pairs = [(q_rows[DH * (h % 2):DH * (h % 2) + DH, (h // 2) * P:(h // 2 + 1) * P],
                          k_rows[DH * (h % 2):DH * (h % 2) + DH, (h // 2) * P:(h // 2 + 1) * P]) for h in heads]
                jobs.append((("product", pairs), None, SCALE,
                             m_hi[:, heads[0]:heads[-1] + 1:2, :], m_lo[:, heads[0]:heads[-1] + 1:2, :]))
            if layer:
                for c in range(2):
                    jobs.append((None, raw_b[:, 2, c * 512:(c + 1) * 512], 1.0,
                                 v_hi[:, c * 512:(c + 1) * 512], v_lo[:, c * 512:(c + 1) * 512]))
                for c in range(2):
                    jobs.append((None, raw_b[:, 3, c * 512:(c + 1) * 512], 1.0,
                                 o_hi[:, 4 * c:4 * c + 4, :].rearrange("p a n -> p (a n)"),
                                 o_lo[:, 4 * c:4 * c + 4, :].rearrange("p a n -> p (a n)")))
            return jobs

        def ffn_jobs():
            jobs = []
            for w, (hi, lo) in enumerate(((g_hi, g_lo), (u_hi, u_lo), (d_hi, d_lo))):
                for a, b in ((0, 4), (4, 8), (8, 9)):
                    jobs.append((None, raw_f[:, w, a:b, :].rearrange("p a n -> p (a n)"), 1.0,
                                 hi[:, a:b, :].rearrange("p a n -> p (a n)"), lo[:, a:b, :].rearrange("p a n -> p (a n)")))
            jobs.append((None, raw_r[:, :], 1.0, r_hi[:, :], r_lo[:, :]))
            return jobs

        JOBS = [attention_jobs(0), ffn_jobs(), attention_jobs(1)]
        PRODUCTS = 4
        JOB_START = [0, len(JOBS[0]), len(JOBS[0]) + len(JOBS[1])]
        MADE_START = [0, len(JOBS[0]), len(JOBS[0])]

        def prep_pe(eng, stage):
            for i, (work, *_) in enumerate(JOBS[stage]):
                if work is None:
                    continue
                bank = banks[i % 4]
                if i >= 4 and JOBS[stage][i - 4][0] is not None:
                    eng.wait_ge(prep_lo, JOB_START[stage] + i - 3)
                for j, piece in enumerate(work[1]):
                    dst = bank[:, j * P:(j + 1) * P]
                    if work[0] == "turn":
                        last = eng.transpose(dst, piece, ident[:, :])
                    else:
                        last = eng.matmul(dst, piece[0], piece[1], start=True, stop=True)
                last.then_inc(prep_made, 1)

        def job_source(stage, i):
            work, src, _, hi, _ = JOBS[stage][i]
            if work is None:
                return src
            if work[0] == "product":
                return banks[i % 4][:, :].rearrange("p (a n) -> p a n", a=4)
            return banks[i % 4][:, :]

        def prep_act(eng, stage, first=0, last=None):
            for i, (work, _, scale, hi, _) in list(enumerate(JOBS[stage]))[first:last]:
                if work is not None:
                    eng.wait_ge(prep_made, MADE_START[stage] + i + 1)
                eng.activation(hi, job_source(stage, i), ACT.Copy, scale=scale).then_inc(prep_hi, 1)

        def prep_dve(eng, stage, first=0, last=None):
            for i, (work, _, scale, hi, lo) in list(enumerate(JOBS[stage]))[first:last]:
                eng.wait_ge(prep_hi, JOB_START[stage] + i + 1)
                eng.scalar_tensor_tensor(out=lo, in0=job_source(stage, i), scalar=scale, in1=hi.bitcast(F32),
                                         op0=ALU.mult, op1=ALU.subtract).then_inc(prep_lo, 1)

        def prepared(eng, stage):
            eng.wait_ge(prep_lo, JOB_START[stage] + len(JOBS[stage]))

        def turn_raw_pe(eng):
            eng.wait_ge(loaded_b, 4 * 16)
            for c in range(4):
                for j in range(4):
                    last = eng.transpose(banks[c][:, j * P:(j + 1) * P],
                                         raw_b[:, c // 2, ((c % 2) * 4 + j) * P:((c % 2) * 4 + j + 1) * P], ident[:, :])
                last.then_inc(prep_turned, 1)

        def turn_raw_act(eng):
            for c in range(4):
                eng.wait_ge(prep_turned, 4)
                eng.activation(raw_turned[:, c * 512:(c + 1) * 512], banks[c][:, :], ACT.Copy)\
                   .then_inc(prep_turned, 1)

        @block.sync
        def _(eng):
            x_tiles = x_in.rearrange("b (t p) d -> p (b t) d", p=P)
            eng.dma_start(x[:, 0:TILES, :], x_tiles[:, 0:TILES, :]).then_inc(loaded_first, 16)
            eng.dma_start(raw_a[:, 0, :].rearrange("p (j d) -> p j d", d=P), wq_a.rearrange("(j g) q d -> (g q) j d", g=2)).then_inc(loaded_a, 16)
            eng.dma_start(raw_a[:, 1, :].rearrange("p (j d) -> p j d", d=P), wk_a.rearrange("(j g) q d -> (g q) j d", g=2)).then_inc(loaded_a, 16)
            eng.dma_start(x[:, TILES:, :], x_tiles[:, TILES:, :]).then_inc(loaded_x, 16)
            eng.dma_start(raw_f[:, 0, 0:FPAIRS, :].rearrange("p a (g f) -> p (a g) f", g=2), wg.rearrange("e d f -> d e f")).then_inc(loaded_f, 16)
            eng.dma_start(raw_f[:, 1, 0:FPAIRS, :].rearrange("p a (g f) -> p (a g) f", g=2), wu.rearrange("e d f -> d e f")).then_inc(loaded_f, 16)
            eng.dma_start(raw_f[:, 2, 0:FPAIRS, :], wd.rearrange("(a g) f d -> (g f) a d", g=2)).then_inc(loaded_f, 16)
            for w, part in enumerate((sg, su, sd)):
                eng.dma_start(raw_f[:, w, FPAIRS, :], part).then_inc(loaded_f, 16)
            eng.dma_start(raw_r[:, :], wr).then_inc(loaded_f, 16)
            for w, part in enumerate((wq_b, wk_b, wv_b)):
                eng.dma_start(raw_b[:, w, :], part).then_inc(loaded_b, 16)
            eng.dma_start(raw_b[:, 3, :].rearrange("p (j n) -> p j n", n=P), wo_b.rearrange("(j p) n -> p j n", p=P)).then_inc(loaded_b, 16)

            o_tiles = out.rearrange("b (t p) d -> p (b t) d", p=P)
            for w in range(FUNITS):
                done = FL + 2 + MISC_USES * (w + 1) + (3 if w < FUNITS - 2 else 1) if w < FUNITS - 1 else 2 * FL
                eng.wait_ge(misc_free, done)
                eng.dma_start(o_tiles[:, FTILES * w:FTILES * (w + 1), :], x[:, FTILES * w:FTILES * (w + 1), :]).then_inc(stored, 16)
            eng.wait_ge(stored, 16 * FUNITS)

        @block.gpsimd
        def _(eng):
            eng.memset(ident[:, :], 0.0).then_inc(consts, 1)
            eng.memset(ident_b[:, :], 0.0).then_inc(consts, 1)
            eng.memset(zero[:, :], 0.0).then_inc(consts, 1)
            eng.memset(causal[:, :], 0.0).then_inc(consts, 1)
            eng.memset(select[:, :, :], 0.0).then_inc(consts, 1)
            eng.memset(cw_parts[:, :, :, :], 0.0).then_inc(consts, 1)
            eng.wait_ge(consts, 6)
            for m in (ident, ident_b):
                eng.affine_select(out=m[:, :], in_=m[:, :], compare_op=ALU.not_equal, fill=1.0, base=0,
                                  pattern=[[-1, P]], channel_multiplier=1).then_inc(consts, 1)
            eng.affine_select(out=causal[:, :], in_=causal[:, :], compare_op=ALU.is_ge, fill=NEG, base=0,
                              pattern=[[-1, P]], channel_multiplier=1).then_inc(consts, 1)
            eng.memset(prob_w[:, :, :], NONE).then_inc(consts, 1)
            for part in range(3):
                view = select[:, :, :].rearrange("p a (g f) -> p a g f", g=2)
                eng.affine_select(out=view, in_=view, compare_op=ALU.not_equal, fill=1.0, base=-EXPERTS * part,
                                  pattern=[[-2, FPAIRS], [-1, 2], [0, DH]], channel_multiplier=1).then_inc(consts, 1)
                eng.wait_ge(consts, 10 + part + 1)

            def scale(layer, unit, h):
                n = unit.count(HEADS, BATCH * HEADS * layer + h)
                eng.wait_ge(rec_done, n + 1)
                if layer:
                    last = eng.tensor_tensor(probs[:, h % 4, :, :], probs[:, h % 4, :, :],
                                             rec[:, h % 4, :].unsqueeze(2).to_broadcast([P, TILES, SEQ]), ALU.mult)
                else:
                    for t in range(TILES):
                        part = probs[:, h % 4, t, 0:(t + 1) * P]
                        last = eng.tensor_tensor(part, part, rec[:, h % 4, t:t + 1].to_broadcast([P, (t + 1) * P]), ALU.mult)
                last.then_inc(scaled, 1)

            def split(layer, unit, c, wait_out):
                b = unit.count(PAIRS, BATCH * PAIRS * layer + c - PAIRS)
                slot = 1 - unit.par
                if layer == 0:
                    eng.wait_ge(heads_taken, b + 1)
                else:
                    eng.wait_ge(gelu_done, unit.count(2, -2 + c // 4 + 1))
                if wait_out is not None:
                    eng.wait_ge(side_made, wait_out)
                eng.tensor_tensor(cat_hi[:, c, :], cat[:, slot, c, :], zero[:, :].to_broadcast([P, SEQ]), ALU.subtract).then_inc(cat_hi_done, 1)
                eng.wait_ge(cat_hi_done, b + 1)
                eng.tensor_tensor(cat_lo[:, c, :], cat[:, slot, c, :], cat_hi[:, c, :].bitcast(F32), ALU.subtract)\
                   .then_inc(cat_lo_done, 1)

            def pool_attention(layer):
                for h in range(S_AHEAD - 2):
                    scale(layer, Unit(0, 0), h)

                def unit_work(unit):
                    for h in range(HEADS):
                        if h + S_AHEAD - 2 < HEADS or not unit.last:
                            scale(layer, unit, h + S_AHEAD - 2)
                        if not unit.first and h in SPLITS:
                            c = SPLITS[h]
                            out_before = None
                            if c == 0 and not (isinstance(unit.it, int) and 2 * unit.it + unit.c < 2):
                                out_before = side_use(layer, unit, ("out", 0)) - SIDE_USES + 1
                            split(layer, unit, c, out_before)
                each_unit(eng, BATCH, unit_work)
                last = Unit(BATCH // 2 - 1, 1, last=True)
                for c in range(PAIRS):
                    split(layer, END, c, side_use(layer, last, ("out", 0)) + 1 if c == 0 else None)

            def pool_ffn(layer):
                def unit_work(unit):
                    for f in range(FBLOCKS):
                        k = unit.count(FBLOCKS, FUNITS * FBLOCKS * layer + f)
                        slot = (unit.par * FBLOCKS + f) % 3
                        eng.wait_ge(hid_hi_done, k + 1)
                        eng.tensor_tensor(hid_lo[:, slot, :], hid[:, slot, :], hid_hi[:, slot, :].bitcast(F32), ALU.subtract)\
                           .then_inc(hid_lo_done, 1)
                each_unit(eng, FUNITS, unit_work)

            pool_attention(0)
            pool_ffn(0)
            pool_attention(1)
            pool_ffn(1)

        @block.scalar
        def _(eng):
            eng.dma_start(raw_a[:, 2, :].rearrange("p (j d) -> p j d", d=P), wv_a.rearrange("(j g) v d -> (g v) j d", g=2)).then_inc(loaded_a, 16)
            eng.dma_start(raw_a[:, 3, :], wo_a).then_inc(loaded_a, 16)

            def take_x(layer, unit, slot):
                eng.wait_ge(side_made, side_use(layer, unit, ("x_t", 0)) + 1)
                eng.activation(xt_hi[:, slot, 0:SEQ], side[:, 0:SEQ], ACT.Copy).then_inc(xt_hi_done, 1)

            def take_v(layer, unit, i, slot):
                eng.wait_ge(side_made, side_use(layer, unit, ("v", i)) + 1)
                eng.activation(values[:, slot, i // 2, (i % 2) * 512:(i % 2 + 1) * 512], side[:, :], ACT.Copy)\
                   .then_inc(side_free, 1)

            def take_y(layer, unit, h):
                n = unit.count(HEADS, BATCH * HEADS * layer + h)
                eng.wait_ge(y_made, n + 1)
                eng.activation(y_hi[:, h % 2, :], proj[:, 0:SEQ], ACT.Copy).then_inc(y_hi_done, 1)

            def exps(layer, unit, h):
                n = unit.count(HEADS, BATCH * HEADS * layer + h)
                eng.wait_ge(max_done, n + 1)
                for t in range(TILES):
                    keys = SEQ if layer else (t + 1) * P
                    last = eng.activation(probs[:, h % 4, t, 0:keys], score[h % 4][:, t * SEQ:t * SEQ + keys], ACT.Exp,
                                          bias=negmax[:, h % 4, t:t + 1], accum_out=sums[:, h % 4, t:t + 1])
                last.then_inc(exp_done, 1)

            def take_heads(layer, unit, p):
                eng.wait_ge(heads_made, unit.count(PAIRS, BATCH * PAIRS * layer + p) + 1)
                if p == 0:
                    wait(eng, cat_lo_done, unit.count(PAIRS, BATCH * PAIRS * layer - PAIRS))
                slot = unit.par if p >= 0 else 1 - unit.par
                eng.activation(cat[:, slot, p % PAIRS, :], heads_out[:, 0:SEQ], ACT.Copy).then_inc(heads_taken, 1)

            def gelu(unit):
                slot = 1 - unit.par
                eng.wait_ge(heads_taken, unit.count(PAIRS, BATCH * PAIRS))
                for half in range(2):
                    part = cat[:, slot, 4 * half:4 * half + 4, :]
                    eng.activation(part, part, ACT.Gelu).then_inc(gelu_done, 1)

            def take_out(layer, unit):
                eng.wait_ge(side_made, side_use(layer, unit, ("out", 0)) + 1)
                eng.activation(out_s[:, :], side[:, 0:SEQ], ACT.Copy).then_inc(side_free, 1)

            def act_attention(layer):
                start = Unit(0, 0, first=True)
                take_x(layer, None, 0)
                if layer:
                    act_ffn(0)[2]()
                for i in range(0, V_PARTS, 2):
                    take_v(layer, None, i, 0)
                for e, i in PROLOGUE:
                    if e == "y":
                        take_y(layer, start, i)
                    elif e == "scores":
                        exps(layer, start, i)

                def unit_work(unit):
                    for h, step in enumerate(attention_stream(unit.first, unit.last)):
                        if ("out", O_PARTS - 1) in step:
                            take_out(layer, unit)
                        for i in range(V_PARTS):
                            if ("v", i) in step:
                                take_v(layer, unit, i, 1 - unit.par)
                        if ("y", h + Y_AHEAD) in step:
                            take_y(layer, unit, h + Y_AHEAD)
                        if ("scores", h + S_AHEAD) in step:
                            exps(layer, unit, h + S_AHEAD)
                        if ("av", h // 2 - 1) in step:
                            take_heads(layer, unit, h // 2 - 1)
                        if layer and not unit.first and h == 1:
                            gelu(unit)
                        if ("x_t", 0) in step:
                            take_x(layer, unit, 1 - unit.par)
                        if not layer and unit.first and h < len(JOBS[1]):
                            if h == 0:
                                eng.wait_ge(loaded_f, 7 * 16)
                            prep_act(eng, 1, h, h + 1)
                each_unit(eng, BATCH, unit_work)
                take_heads(layer, END, -1)
                start_ffn, ffn_units, _ = act_ffn(layer)
                if layer:
                    gelu(END)
                start_ffn()
                take_out(layer, END)
                ffn_units()

            def act_ffn(layer):
                def take_fx(unit, slot):
                    eng.wait_ge(misc_made, misc_use(layer, unit, "x") + 1)
                    eng.activation(xt_hi[:, slot, :], misc[:, :], ACT.Copy).then_inc(fxt_hi_done, 1)

                def router(unit):
                    eng.wait_ge(misc_free, misc_use(layer, unit, "logits") + 1)
                    eng.activation(prob_r[:, 1, :, :], prob_r[:, 0, :, :], ACT.Exp).then_inc(router_exp, 1)

                def take_cw(unit, slot):
                    use_no = misc_use(layer, unit, "cw")
                    eng.wait_ge(misc_made, use_no + 1)
                    eng.activation(cw_t[:, slot, :], misc_b[0:3 * EXPERTS, 0:FTOK], ACT.Copy).then_inc(misc_free, 1)

                def silus(unit, f):
                    k = unit.count(FBLOCKS, FUNITS * FBLOCKS * layer + f)
                    slot = (unit.par * FBLOCKS + f) % 2
                    eng.wait_ge(gate_made, k + 1)
                    wait(eng, gated, k - 1)
                    eng.activation(silu[:, slot, :], gate[slot][:, :], ACT.Silu).then_inc(silu_done, 1)

                def high(unit, f):
                    k = unit.count(FBLOCKS, FUNITS * FBLOCKS * layer + f)
                    slot = (unit.par * FBLOCKS + f) % 3
                    if f % FBLOCKS == FBLOCKS - 1:
                        eng.wait_ge(gated, k + 1)
                    else:
                        eng.wait_ge(weighted, weights_before(layer, unit, f) + 1)
                    wait(eng, down_made, k - 2)
                    eng.activation(hid_hi[:, slot, :], hid[:, slot, :], ACT.Copy).then_inc(hid_hi_done, 1)

                def take_fout(unit):
                    eng.wait_ge(down_made, unit.count(FBLOCKS, FUNITS * FBLOCKS * layer))
                    eng.activation(fout_s, acc[:, :], ACT.Copy).then_inc(fout_done, 1)

                def start_ffn():
                    take_fx(None, 0)
                    if not layer:
                        turn_raw_act(eng)
                    router(None)
                    if not layer:
                        prep_act(eng, 2, 0, PRODUCTS)

                def unit_work(unit):
                    for f in range(FBLOCKS):
                        if f == DOWN_LAG and not unit.first:
                            take_fout(unit)
                        silus(unit, f)
                        if f >= HIGH_LAG or not unit.first:
                            high(unit, f - HIGH_LAG)
                        if f == 0:
                            take_cw(unit, unit.par)
                        if f == 4 and not unit.last:
                            take_fx(unit, 1 - unit.par)
                        if f == 5 and not unit.last:
                            router(unit)
                        if not layer and unit.first and f < len(JOBS[2]) - PRODUCTS:
                            prep_act(eng, 2, PRODUCTS + f, PRODUCTS + f + 1)

                def ffn_units():
                    each_unit(eng, FUNITS, unit_work)
                    for f in range(HIGH_LAG):
                        high(FEND, f - HIGH_LAG)

                return start_ffn, ffn_units, lambda: take_fout(FEND)

            eng.wait_ge(loaded_a, 4 * 16)
            prep_act(eng, 0)
            act_attention(0)
            act_attention(1)
            act_ffn(1)[2]()

        @block.tensor
        def _(eng):
            def claim(layer, unit, event):
                wait(eng, side_free, side_use(layer, unit, event))

            def three(dst, a_hi, a_lo, b_hi, b_lo, start=True, stop=True, masked=None):
                eng.matmul(dst, a_hi, b_hi, start=start, stop=False)
                if masked is not None:
                    eng.matmul(masked, ident_b[:, :], causal[:, :], start=False, stop=False, skip_group_check=True)
                eng.matmul(dst, a_hi, b_lo, start=False, stop=False)
                return eng.matmul(dst, a_lo, b_hi, start=False, stop=stop)

            def attention(layer):
                def x_t(unit, number):
                    claim(layer, unit, ("x_t", 0))
                    eng.wait_ge(xn_done, number)
                    for t in range(TILES):
                        last = eng.transpose(side[:, t * P:(t + 1) * P], xn[:, t, :], ident[:, :])
                    last.then_inc(side_made, 1)

                def v(unit, i, slot):
                    claim(layer, unit, ("v", i))
                    tok = slice((i // 2) * P, (i // 2 + 1) * P)
                    cols = slice((i % 2) * 512, (i % 2 + 1) * 512)
                    three(side[:, :], xt_hi[:, slot, tok], xt_lo[:, slot, tok], v_hi[:, cols], v_lo[:, cols])\
                        .then_inc(side_made, 1)

                def y(unit, h):
                    n = unit.count(HEADS, BATCH * HEADS * layer + h)
                    slot = (unit.par + h // HEADS) % 2
                    wait(eng, y_lo_done, n)
                    three(proj[:, 0:SEQ], m_hi[:, h % HEADS, :], m_lo[:, h % HEADS, :],
                          xt_hi[:, slot, 0:SEQ], xt_lo[:, slot, 0:SEQ]).then_inc(y_made, 1)

                def scores(unit, h):
                    n = unit.count(HEADS, BATCH * HEADS * layer + h)
                    slot = (unit.par + h // HEADS) % 2
                    eng.wait_ge(y_lo_done, n + 1)
                    wait(eng, exp_done, n - 3)
                    for t in range(TILES):
                        keys = SEQ if layer else (t + 1) * P
                        dst = score[h % 4][:, t * SEQ:t * SEQ + keys]
                        q = slice(t * P, (t + 1) * P)
                        diagonal = None if layer else score[h % 4][:, t * SEQ + t * P:t * SEQ + (t + 1) * P]
                        last = three(dst, y_hi[:, h % 2, q], y_lo[:, h % 2, q], xt_hi[:, slot, 0:keys], xt_lo[:, slot, 0:keys],
                                     masked=diagonal)
                    last.then_inc(score_made, 1)

                def probs_turned(unit, h):
                    n = unit.count(HEADS, BATCH * HEADS * layer + h)
                    eng.wait_ge(scaled, n + 1)
                    wait(eng, turn_done, n)
                    for k in range(TILES):
                        for q in range(TILES):
                            if layer or k <= q:
                                last = eng.transpose(turn[:, turned(layer, k, q)],
                                                     probs[:, h % 4, q, k * P:(k + 1) * P], ident[:, :])
                    last.then_inc(turn_made, 1)

                def av(unit, p):
                    wait(eng, heads_taken, unit.count(PAIRS, BATCH * PAIRS * layer + p))
                    eng.wait_ge(turn_done, unit.count(HEADS, BATCH * HEADS * layer + 2 * p + 2))
                    slot = unit.par if p >= 0 else 1 - unit.par
                    for k in range(TILES):
                        q0 = 0 if layer else k * P
                        for g in range(2):
                            h = (2 * p + g) % HEADS
                            last = eng.matmul(heads_out[DH * g:DH * g + DH, q0:SEQ],
                                              values[:, slot, k, h * DH:(h + 1) * DH],
                                              probs_t[:, h % 4, turned(layer, k, q0 // P).start:turned(layer, k, TILES - 1).stop], start=(k == 0), stop=(k == TILES - 1),
                                              skip_group_check=True)
                    last.then_inc(heads_made, 1)

                def out(unit, i, b):
                    each = PAIRS // O_PARTS
                    if i == 0:
                        claim(layer, unit, ("out", 0))
                    eng.wait_ge(cat_lo_done, b + each * (i + 1))
                    for j in range(each * i, each * (i + 1)):
                        last = three(side[:, 0:SEQ], o_hi[:, j, :], o_lo[:, j, :], cat_hi[:, j, :], cat_lo[:, j, :],
                                     start=(j == 0), stop=(j == PAIRS - 1))
                    if i == O_PARTS - 1:
                        last.then_inc(side_made, 1)

                def out_t(unit):
                    claim(layer, unit, ("out_t", 0))
                    for t in range(TILES):
                        last = eng.transpose(side[:, t * P:(t + 1) * P], out_s[:, t * P:(t + 1) * P], ident[:, :])
                    last.then_inc(side_made, 1)

                start = Unit(0, 0, first=True)
                for e, i in PROLOGUE:
                    if e == "x_t":
                        x_t(None, BATCH * layer + 1)
                    elif e == "v":
                        v(None, i, 0)
                        if layer and i == V_PARTS - 1:
                            ffn(0)[2]()
                    elif e == "y":
                        y(start, i)
                    else:
                        scores(start, i)
                if layer:
                    before_ffn_end(eng, 0)

                def unit_work(unit):
                    for step in attention_stream(unit.first, unit.last):
                        for e, i in step:
                            if e == "probs_t":
                                probs_turned(unit, i)
                            elif e == "y":
                                y(unit, i)
                            elif e == "scores":
                                scores(unit, i)
                            elif e == "av":
                                av(unit, i)
                            elif e == "out":
                                out(unit, i, unit.count(PAIRS, BATCH * PAIRS * layer - PAIRS))
                            elif e == "out_t":
                                out_t(unit)
                            elif e == "x_t":
                                x_t(unit, unit.count(1, BATCH * layer + 2))
                            else:
                                v(unit, i, 1 - unit.par)
                each_unit(eng, BATCH, unit_work)
                av(END, -1)
                start_ffn, ffn_units, _ = ffn(layer)
                start_ffn()
                for i in range(O_PARTS):
                    out(END, i, BATCH * PAIRS * (layer + 1) - PAIRS)
                out_t(END)
                before_layer(eng, layer)
                if not layer:
                    eng.wait_ge(prep_lo, JOB_START[2] + PRODUCTS)
                ffn_units()

            def ffn(layer):
                def x_t(unit, number):
                    no = misc_use(layer, unit, "x")
                    wait(eng, misc_free, no)
                    eng.wait_ge(fxn_done, number)
                    for t in range(FTILES):
                        last = eng.transpose(misc[:, t * P:(t + 1) * P], xn[:, t, :], ident[:, :])
                    last.then_inc(misc_made, 1)

                def logits(unit, slot):
                    no = misc_use(layer, unit, "logits")
                    eng.wait_ge(misc_free, no)
                    for t in range(FTILES):
                        tok = slice(t * P, (t + 1) * P)
                        last = three(misc[:, t * EXPERTS:(t + 1) * EXPERTS], xt_hi[:, slot, tok], xt_lo[:, slot, tok],
                                     r_hi[:, :], r_lo[:, :])
                    last.then_inc(misc_made, 1)

                def cw_turned(unit, number):
                    no = misc_use(layer, unit, "cw")
                    eng.wait_ge(misc_free, no)
                    eng.wait_ge(cw_done, number)
                    for t in range(FTILES):
                        last = eng.transpose(misc_b[:, t * P:(t + 1) * P],
                                             cw_parts[:, t, :, :].rearrange("p a e -> p (a e)"), ident_b[:, :])
                    last.then_inc(misc_made, 1)

                def blocks(unit, f):
                    k = unit.count(FBLOCKS, FUNITS * FBLOCKS * layer + f)
                    b = (unit.par * FBLOCKS + f) % 2
                    xs = xt_hi[:, unit.par, :], xt_lo[:, unit.par, :]
                    wait(eng, silu_done, k - 1)
                    three(gate[b][:, :], g_hi[:, f, :], g_lo[:, f, :], *xs).then_inc(gate_made, 1)
                    wait(eng, gated, k - 1)
                    three(up[b][:, :], u_hi[:, f, :], u_lo[:, f, :], *xs).then_inc(up_made, 1)

                def spreads(unit, f):
                    if f == 0:
                        eng.wait_ge(misc_free, misc_use(layer, unit, "cw") + 1)
                    wait(eng, weighted, weights_before(layer, unit, f) - 1)
                    eng.matmul(spread[f % 2][:, :], select[:, f, :], cw_t[:, unit.par, :], start=True, stop=True)\
                       .then_inc(spread_made, 1)

                def down(unit, f):
                    k = unit.count(FBLOCKS, FUNITS * FBLOCKS * layer + f)
                    slot = (unit.par * FBLOCKS + f) % 3
                    f %= FBLOCKS
                    if f == 0:
                        wait(eng, fout_done, unit.count(1, FUNITS * layer))
                    eng.wait_ge(hid_lo_done, k + 1)
                    three(acc[:, :], d_hi[:, f, :], d_lo[:, f, :], hid_hi[:, slot, :], hid_lo[:, slot, :],
                          start=(f == 0), stop=(f == FBLOCKS - 1)).then_inc(down_made, 1)

                def out_t(unit, number):
                    no = misc_use(layer, unit, "out")
                    eng.wait_ge(misc_free, no)
                    eng.wait_ge(fout_done, number)
                    for t in range(FTILES):
                        last = eng.transpose(misc[:, t * P:(t + 1) * P], fout_s[:, t * P:(t + 1) * P], ident[:, :])
                    last.then_inc(misc_made, 1)

                def start_ffn():
                    prepared(eng, 1)
                    x_t(None, FUNITS * layer + 1)
                    if not layer:
                        turn_raw_pe(eng)
                    logits(None, 0)
                    if not layer:
                        eng.wait_ge(prep_turned, 8)
                        prep_pe(eng, 2)

                def unit_work(unit):
                    for f in range(FBLOCKS):
                        blocks(unit, f)
                        if f == 4 and not unit.last:
                            x_t(unit, unit.count(1, FUNITS * layer + 2))
                        if f:
                            spreads(unit, f - 1)
                        if f >= DOWN_LAG or not unit.first:
                            down(unit, f - DOWN_LAG)
                        if f == 0:
                            cw_turned(unit, unit.count(1, FUNITS * layer + 1))
                        if not unit.last:
                            if f == 5:
                                logits(unit, 1 - unit.par)
                        if f == 7 and not unit.first:
                            out_t(unit, unit.count(1, FUNITS * layer))

                def ffn_units():
                    each_unit(eng, FUNITS, unit_work)
                    for f in range(DOWN_LAG):
                        down(FEND, f - DOWN_LAG)

                return start_ffn, ffn_units, lambda: out_t(FEND, FUNITS * (layer + 1))

            eng.wait_ge(consts, 13)
            eng.wait_ge(loaded_a, 4 * 16)
            prep_pe(eng, 0)
            prepared(eng, 0)
            attention(0)
            prepared(eng, 2)
            attention(1)
            ffn(1)[2]()

        @block.vector
        def _(eng):
            class Chain:

                def __init__(self):
                    self.base, self.k = 0, 0

                def at(self, value):
                    self.base, self.k = value, 0

                def link(self, ins):
                    ins.then_inc(dve_chain, 1)
                    self.k += 1
                    eng.wait_ge(dve_chain, self.base + self.k)

            chain = Chain()
            def tiles_of(unit, ahead, tiles):
                if unit is None:
                    return x[:, 0:tiles, :]
                at = unit.count(tiles, ahead * tiles)
                return x[:, at:at + tiles, :] if isinstance(at, int) else x[:, bass.ds(at, tiles), :]

            NORM_PARTS = 5
            NORM = 16

            def normalise(src, tiles, part, done):
                mean, diff, both = (moments[:, i, 0:tiles] for i in range(3))
                v, r, a, b = var[:, 0:tiles], newton[:, 0, 0:tiles], newton[:, 1, 0:tiles], newton[:, 2, 0:tiles]
                if part == 0:
                    for t in range(tiles):
                        last = eng.bn_stats(stats[:, t, :], src[:, t, :])
                    chain.link(last)
                    even, odd = stats[:, 0:tiles, 1], stats[:, 0:tiles, 4]
                    eng.tensor_tensor(mean, even, odd, ALU.add)
                    eng.tensor_tensor(diff, even, odd, ALU.subtract)
                    chain.link(eng.tensor_tensor(both, stats[:, 0:tiles, 2], stats[:, 0:tiles, 5], ALU.add))
                    eng.tensor_scalar(mean, mean, 0.5, None, ALU.mult)
                    chain.link(eng.scalar_tensor_tensor(out=diff, in0=diff, scalar=0.25, in1=diff, op0=ALU.mult, op1=ALU.mult))
                    chain.link(eng.scalar_tensor_tensor(out=both, in0=both, scalar=1.0 / P, in1=diff, op0=ALU.mult, op1=ALU.add))
                if part == 1:
                    chain.link(eng.tensor_scalar(v, both, EPS, None, ALU.add))
                    chain.link(eng.tensor_scalar(a.bitcast(I32), v.bitcast(I32), 1, None, ALU.logical_shift_right))
                    chain.link(eng.tensor_scalar(r.bitcast(I32), a.bitcast(I32), -1.0, float(0x5F3759DF), ALU.mult, ALU.add))
                if part in (1, 2, 3):
                    chain.link(eng.scalar_tensor_tensor(out=a, in0=r, scalar=-0.5, in1=r, op0=ALU.mult, op1=ALU.mult))
                    chain.link(eng.tensor_tensor(b, a, v, ALU.mult))
                    chain.link(eng.scalar_tensor_tensor(out=r, in0=b, scalar=1.5, in1=r, op0=ALU.add, op1=ALU.mult))
                if part == 4:
                    for t in range(tiles):
                        last = eng.tensor_scalar(xn[:, t, :], src[:, t, :], mean[:, t:t + 1], r[:, t:t + 1],
                                                 ALU.subtract, ALU.mult)
                    last.then_inc(done, 1)

            def add_normalised(layer, unit, tiles, number):
                if layer:
                    eng.wait_ge(xn_done, number)
                    chain.link(eng.tensor_tensor(tiles, tiles, xn[:, 0:TILES, :], ALU.add))

            def low_x(layer, unit, slot, number):
                eng.wait_ge(xt_hi_done, number)
                eng.tensor_tensor(xt_lo[:, slot, 0:SEQ], side[:, 0:SEQ], xt_hi[:, slot, 0:SEQ].bitcast(F32),
                                  ALU.subtract).then_inc(side_free, 1)

            def take_v(layer, unit, i, slot):
                eng.wait_ge(side_made, side_use(layer, unit, ("v", i)) + 1)
                eng.tensor_copy(values[:, slot, i // 2, (i % 2) * 512:(i % 2 + 1) * 512], side[:, :])\
                   .then_inc(side_free, 1)

            def low_y(layer, unit, h):
                n = unit.count(HEADS, BATCH * HEADS * layer + h)
                eng.wait_ge(y_hi_done, n + 1)
                eng.tensor_tensor(y_lo[:, h % 2, :], proj[:, 0:SEQ], y_hi[:, h % 2, :].bitcast(F32),
                                  ALU.subtract).then_inc(y_lo_done, 1)

            def maxima(layer, unit, h):
                n = unit.count(HEADS, BATCH * HEADS * layer + h)
                eng.wait_ge(score_made, n + 1)
                if layer:
                    last = eng.tensor_reduce(negmax[:, h % 4, :], score[h % 4][:, :].rearrange("p (t k) -> p t k", t=TILES),
                                             AX.X, ALU.max, negate=True)
                else:
                    for t in range(TILES):
                        last = eng.tensor_reduce(negmax[:, h % 4, t:t + 1], score[h % 4][:, t * SEQ:t * SEQ + (t + 1) * P],
                                                 AX.X, ALU.max, negate=True)
                last.then_inc(max_done, 1)

            def reciprocals(layer, unit, h):
                eng.wait_ge(exp_done, unit.count(HEADS, BATCH * HEADS * layer + h) + 1)
                eng.reciprocal(rec[:, h % 4, :], sums[:, h % 4, :]).then_inc(rec_done, 1)

            def take_probs(layer, unit, h):
                n = unit.count(HEADS, BATCH * HEADS * layer + h)
                eng.wait_ge(turn_made, n + 1)
                cols = turned(layer, TILES - 1, TILES - 1).stop
                eng.tensor_copy(probs_t[:, h % 4, 0:cols], turn[:, 0:cols]).then_inc(turn_done, 1)

            def add_out(layer, unit, tiles):
                eng.wait_ge(side_made, side_use(layer, unit, ("out_t", 0)) + 1)
                eng.tensor_tensor(tiles, tiles, side[:, 0:SEQ].rearrange("p (t d) -> p t d", t=TILES), ALU.add)\
                   .then_inc(side_free, 1)

            def dve_attention(layer):
                start = Unit(0, 0, first=True)
                per, links = NORM + layer, ATTENTION_LINKS[layer]
                low_x(layer, None, 0, BATCH * layer + 1)
                for i in range(1, V_PARTS, 2):
                    take_v(layer, None, i, 0)
                if layer:
                    run_ffn(0)[2]()
                for e, i in PROLOGUE:
                    if e == "y":
                        low_y(layer, start, i)
                    elif e == "scores":
                        maxima(layer, start, i)
                        if i >= 2:
                            reciprocals(layer, start, i - 2)

                def unit_work(unit):
                    for h, step in enumerate(attention_stream(unit.first, unit.last)):
                        take_probs(layer, unit, h)
                        if h + S_AHEAD - 2 < HEADS or not unit.last:
                            reciprocals(layer, unit, h + S_AHEAD - 2)
                        if ("scores", h + S_AHEAD) in step:
                            maxima(layer, unit, h + S_AHEAD)
                        if ("y", h + Y_AHEAD) in step:
                            low_y(layer, unit, h + Y_AHEAD)
                        if h == 0:
                            chain.at(unit.count(per, links + per))
                        if h < NORM_PARTS and not unit.last:
                            normalise(tiles_of(unit, 1, TILES), TILES, h, xn_done)
                        if h == NORM_PARTS - 1 and not unit.last:
                            add_normalised(layer, unit, tiles_of(unit, 1, TILES), unit.count(1, BATCH * layer + 2))
                        if h < NORM_PARTS and unit.last:
                            normalise(tiles_of(None, 0, FTILES), FTILES, h, fxn_done)
                        if not layer and unit.first and h < len(JOBS[1]):
                            prep_dve(eng, 1, h, h + 1)
                        if ("x_t", 0) in step:
                            low_x(layer, unit, 1 - unit.par, unit.count(1, BATCH * layer + 2))
                        if ("out_t", 0) in step:
                            add_out(layer, unit, tiles_of(unit, -1, TILES))
                each_unit(eng, BATCH, unit_work)
                start_ffn, ffn_units, _ = run_ffn(layer)
                start_ffn()
                add_out(layer, END, x[:, (BATCH - 1) * TILES:BATCH * TILES, :])
                ffn_units()

            def dve_ffn(layer):
                def low_fx(unit, slot, number):
                    eng.wait_ge(fxt_hi_done, number)
                    eng.tensor_tensor(xt_lo[:, slot, :], misc[:, :], xt_hi[:, slot, :].bitcast(F32), ALU.subtract)\
                       .then_inc(misc_free, 1)

                def shift_logits(unit):
                    eng.wait_ge(misc_made, misc_use(layer, unit, "logits") + 1)
                    lg = misc[:, 0:FTILES * EXPERTS].rearrange("p (t e) -> p t e", e=EXPERTS)
                    chain.link(eng.tensor_reduce(top[:, 0, :], lg, AX.X, ALU.max))
                    eng.tensor_tensor(prob_r[:, 0, :, :], lg, wide_top(0), ALU.subtract).then_inc(misc_free, 1)

                def wide_top(i):
                    return top[:, i, :].unsqueeze(2).to_broadcast([P, FTILES, EXPERTS])

                e, kept = prob_r[:, 1, :, :], prob_r[:, 2, :, :]
                p, rest = prob_w[:, :, 0:EXPERTS], rest_w[:, :, 0:EXPERTS]

                def router_softmax(number):
                    eng.wait_ge(router_exp, number)
                    chain.link(eng.tensor_reduce(top[:, 0, :], e, AX.X, ALU.add))
                    chain.link(eng.reciprocal(top[:, 1, :], top[:, 0, :]))
                    chain.link(eng.tensor_tensor(p, e, wide_top(1), ALU.mult))

                def carry_wait():
                    eng.memset(carrier[:, :], 0.0)

                def router_pick():
                    carry_wait()
                    for t in range(FTILES):
                        last = eng.max(out=top8[:, t, :], in_=prob_w[:, t, 0:EXPERTS])
                    chain.link(last)
                    chain.link(eng.memset(top8[:, :, 2:TOP8], NONE))
                    carry_wait()
                    for t in range(FTILES):
                        last = eng.match_replace(out=rest_w[:, t, :], in_to_replace=top8[:, t, :],
                                                 in_values=prob_w[:, t, :], imm_value=0.0)
                    chain.link(last)

                def router_parts():
                    chain.link(eng.tensor_tensor(kept, p, rest, ALU.subtract))
                    parts = [cw_parts[:, :, i, :] for i in range(3)]
                    chain.link(eng.tensor_copy(parts[0], kept))
                    chain.link(eng.tensor_tensor(kept, kept, parts[0], ALU.subtract))
                    chain.link(eng.tensor_copy(parts[1], kept))
                    eng.tensor_tensor(parts[2], kept, parts[1], ALU.subtract).then_inc(cw_done, 1)

                def hidden(unit, f):
                    k = unit.count(FBLOCKS, FUNITS * FBLOCKS * layer + f)
                    b = (unit.par * FBLOCKS + f) % 2
                    slot = (unit.par * FBLOCKS + f) % 3
                    eng.wait_ge(silu_done, k + 1)
                    eng.wait_ge(up_made, k + 1)
                    wait(eng, hid_lo_done, k - 2)
                    eng.tensor_tensor(hid[:, slot, :], up[b][:, :], silu[:, b, :], ALU.mult).then_inc(gated, 1)

                def weigh(unit, f):
                    slot = (unit.par * FBLOCKS + f) % 3
                    eng.wait_ge(spread_made, weights_before(layer, unit, f) + 1)
                    eng.wait_ge(gated, unit.count(FBLOCKS, FUNITS * FBLOCKS * layer + f) + 1)
                    eng.tensor_tensor(hid[:, slot, :], spread[f % 2][:, :], hid[:, slot, :], ALU.mult).then_inc(weighted, 1)

                def add_fout(unit, tiles):
                    eng.wait_ge(misc_made, misc_use(layer, unit, "out") + 1)
                    eng.tensor_tensor(tiles, tiles, misc[:, :].rearrange("p (t d) -> p t d", t=FTILES), ALU.add)\
                       .then_inc(misc_free, 1)

                return low_fx, shift_logits, router_softmax, router_pick, router_parts, hidden, weigh, add_fout

            def run_ffn(layer):
                low_fx, shift_logits, router_softmax, router_pick, router_parts, hidden, weigh, add_fout = dve_ffn(layer)
                start = FUNITS * layer
                links = FFN_LINKS[layer]

                def start_ffn():
                    chain.at(links + NORM)
                    low_fx(None, 0, start + 1)
                    shift_logits(None)
                    router_softmax(start + 1)
                    if not layer:
                        prep_dve(eng, 2, 0, PRODUCTS)
                    router_pick()
                    router_parts()
                    assert chain.k == FROUTER, chain.k

                def unit_work(unit):
                    for f in range(FBLOCKS):
                        hidden(unit, f)
                        more = not unit.last
                        if f == 0:
                            chain.at(unit.count(PER, links + PER))
                        ahead = unit.last and not layer
                        if not layer and unit.first and f < len(JOBS[2]) - PRODUCTS:
                            prep_dve(eng, 2, PRODUCTS + f, PRODUCTS + f + 1)
                        for part in {0: (0, 1), 1: (2,), 2: (4,)}.get(f, ()):
                            if more:
                                normalise(tiles_of(unit, 1, FTILES), FTILES, part, fxn_done)
                            if ahead:
                                normalise(tiles_of(None, 0, TILES), TILES, part, xn_done)
                        if ahead and f == 2:
                            add_normalised(1, None, tiles_of(None, 0, TILES), BATCH + 1)
                        if more and f == 7:
                            router_pick()
                        if f == 8 and not unit.first:
                            add_fout(unit, tiles_of(unit, -1, FTILES))
                        if f:
                            weigh(unit, f - 1)
                        if more and f == 1:
                            normalise(tiles_of(unit, 1, FTILES), FTILES, 3, fxn_done)
                        if ahead and f == 1:
                            normalise(tiles_of(None, 0, TILES), TILES, 3, xn_done)
                        if more and f == 4:
                            low_fx(unit, 1 - unit.par, unit.count(1, start + 2))
                        if more and f == 5:
                            shift_logits(unit)
                        if more and f == 6:
                            router_softmax(unit.count(1, start + 2))
                        if more and f == 7:
                            router_parts()
                            assert chain.k == PER, chain.k
                return start_ffn, lambda: each_unit(eng, FUNITS, unit_work),\
                    lambda: add_fout(FEND, x[:, (FUNITS - 1) * FTILES:FUNITS * FTILES, :])

            FROUTER = 1 + 3 + 3 + 4
            PER = NORM + FROUTER
            ATTENTION_LINKS = [0, NORM * BATCH + PER * FUNITS]
            FFN_LINKS = [NORM * BATCH, ATTENTION_LINKS[1] + (NORM + 1) * BATCH]
            eng.wait_ge(loaded_first, 16)
            chain.at(0)
            for part in range(NORM_PARTS):
                normalise(tiles_of(None, 0, TILES), TILES, part, xn_done)
            eng.wait_ge(consts, 13)
            prep_dve(eng, 0)
            eng.wait_ge(loaded_x, 16)
            dve_attention(0)
            dve_attention(1)
            run_ffn(1)[2]()


_INS = ["L0_attn_a_x", "L0_attn_a_w_q", "L0_attn_a_w_k", "L0_attn_a_w_v", "L0_attn_a_w_o", "L0_attn_b_Wq", "L0_attn_b_Wk",
        "L0_attn_b_Wv", "L0_attn_b_Wpost", "L0_ffn_Wr", "L0_ffn_Wg", "L0_ffn_Wu", "L0_ffn_Wd", "L0_ffn_Sg", "L0_ffn_Su",
        "L0_ffn_Sd"]


def kernel(**inputs):
    import numpy as _np
    import concourse.bacc as _bacc
    from concourse import mybir as _mybir
    from concourse.bass_utils import run_bass_kernel_spmd as _run

    nc = _bacc.Bacc("TRN2", target_bir_lowering=False, num_devices=1)
    arrays, args = {}, []
    for name in _INS:
        a = _np.ascontiguousarray(inputs[name])
        arrays[f"in_{name}"] = a
        args.append(nc.dram_tensor(f"in_{name}", a.shape, _mybir.dt.from_np(a.dtype), kind="ExternalInput").ap())
    y = nc.dram_tensor("out_x", (BATCH, SEQ, P), _mybir.dt.float32, kind="ExternalOutput").ap()
    build_program(nc, *args, y)
    r = _run(nc, [arrays], core_ids=[0])
    return r.results[0]["out_x"]
```
